# Optimizing a Trainium2 kernel written in Bass

```python
import numpy as np
import jax
import jax.numpy as jnp

def _softmax(x, axis=-1):
    return jax.nn.softmax(x, axis=axis)

def _gelu(x):
    return jax.nn.gelu(x, approximate=True)

def _silu(x):
    return jax.nn.silu(x)

def _sigmoid(x):
    return jax.nn.sigmoid(x)

def _layernorm(x, axis=-1, eps=1e-05):
    m = jnp.mean(x, axis=axis, keepdims=True)
    v = jnp.var(x, axis=axis, keepdims=True)
    return (x - m) / jnp.sqrt(v + eps)

def _scatter_add(tgt, idx, src, axis=0):
    return tgt.at[idx].add(src)

def _segment_sum(src, seg, n):
    return jax.ops.segment_sum(src, seg, n)
kernel_name = 'mk_macaron_d1_jaxref_r8_fc5962'

def setup_inputs(seed: int=0):
    np.random.seed(seed)
    _w = jnp.asarray

    def _L0_attn_setup():
        import jax, jax.numpy as jnp
        import numpy as np
        B, S, D, H = (2, 256, 128, 16)
        HD = D // H
        MAX_BIAS = 8.0

        def _alibi_bias(T, Sk, dtype):
            slopes = (2.0 ** (-MAX_BIAS / H)) ** jnp.arange(1, H + 1, dtype=dtype)
            qpos = jnp.arange(T)[:, None]
            kpos = jnp.arange(Sk)[None, :]
            rel = -jnp.abs(kpos - qpos).astype(dtype)
            return slopes[:, None, None] * rel[None]
        key = jax.random.key(seed)
        ks = jax.random.split(key, 5)
        sc = 1.0 / np.sqrt(D)
        return {'x': jax.random.normal(ks[0], (B, S, D), jnp.float32), 'Wq': jax.random.normal(ks[1], (D, D), jnp.float32) * sc, 'bq': jnp.zeros((D,), jnp.float32), 'Wk': jax.random.normal(ks[2], (D, D), jnp.float32) * sc, 'bk': jnp.zeros((D,), jnp.float32), 'Wv': jax.random.normal(ks[3], (D, D), jnp.float32) * sc, 'bv': jnp.zeros((D,), jnp.float32), 'Wo': jax.random.normal(ks[4], (D, D), jnp.float32) * sc, 'bo': jnp.zeros((D,), jnp.float32)}
    _L0_attn_in = _L0_attn_setup()

    def _L0_ffn_setup():
        import jax, jax.numpy as jnp
        import numpy as np
        B, T, D, E, TOP_K = (4, 512, 128, 8, 2)
        CAPACITY_FACTOR = 1.5
        key = jax.random.key(seed)
        k1, k2, k3 = jax.random.split(key, 3)
        x = jax.random.normal(k1, (B, T, D), dtype=jnp.float32)
        Wr = jax.random.normal(k2, (E, D), dtype=jnp.float32) * 0.02
        We = jax.random.normal(k3, (E, D, D), dtype=jnp.float32) * 0.02
        return {'x': x, 'Wr': Wr, 'We': We}
    _L0_ffn_in = _L0_ffn_setup()
    _d = {'L0_attn_x': _L0_attn_in['x'], 'L0_attn_Wq': _L0_attn_in['Wq'], 'L0_attn_bq': _L0_attn_in['bq'], 'L0_attn_Wk': _L0_attn_in['Wk'], 'L0_attn_bk': _L0_attn_in['bk'], 'L0_attn_Wv': _L0_attn_in['Wv'], 'L0_attn_bv': _L0_attn_in['bv'], 'L0_attn_Wo': _L0_attn_in['Wo'], 'L0_attn_bo': _L0_attn_in['bo'], 'L0_ffn_Wr': _L0_ffn_in['Wr'], 'L0_ffn_We': _L0_ffn_in['We']}
    _x0 = _d['L0_attn_x']
    _d['L0_attn_x'] = jax.random.normal(jax.random.fold_in(jax.random.key(seed), 1), (16, 512, 128), dtype=_x0.dtype)
    del _x0
    return _d

def reference(L0_attn_x, L0_attn_Wq, L0_attn_bq, L0_attn_Wk, L0_attn_bk, L0_attn_Wv, L0_attn_bv, L0_attn_Wo, L0_attn_bo, L0_ffn_Wr, L0_ffn_We):

    def _L0_attn_ref(x, Wq, bq, Wk, bk, Wv, bv, Wo, bo):
        import jax, jax.numpy as jnp
        import numpy as np
        B, S, D, H = (2, 256, 128, 16)
        HD = D // H
        MAX_BIAS = 8.0

        def _alibi_bias(T, Sk, dtype):
            slopes = (2.0 ** (-MAX_BIAS / H)) ** jnp.arange(1, H + 1, dtype=dtype)
            qpos = jnp.arange(T)[:, None]
            kpos = jnp.arange(Sk)[None, :]
            rel = -jnp.abs(kpos - qpos).astype(dtype)
            return slopes[:, None, None] * rel[None]
        Bb, Ss, Dd = x.shape
        q = (x @ Wq + bq).reshape(Bb, Ss, H, HD)
        k = (x @ Wk + bk).reshape(Bb, Ss, H, HD)
        v = (x @ Wv + bv).reshape(Bb, Ss, H, HD)
        scores = jnp.einsum('bthd,bshd->bhts', q, k) / jnp.sqrt(jnp.asarray(HD, x.dtype))
        alibi = _alibi_bias(Ss, Ss, x.dtype)
        causal = jnp.triu(jnp.ones((Ss, Ss), bool), 1)
        scores = scores + alibi[None]
        scores = jnp.where(causal[None, None], -jnp.inf, scores)
        attn = jax.nn.softmax(scores, axis=-1)
        out = jnp.einsum('bhts,bshd->bthd', attn, v).reshape(Bb, Ss, Dd)
        return out @ Wo + bo

    def _L0_ffn_ref(x, Wr, We):
        import jax, jax.numpy as jnp
        import numpy as np
        B, T, D, E, TOP_K = (4, 512, 128, 8, 2)
        CAPACITY_FACTOR = 1.5
        Bb, Tt, Dd = x.shape
        Ee = Wr.shape[0]
        K = TOP_K
        C = int(Tt * K / Ee * CAPACITY_FACTOR) + 1
        logits = jnp.einsum('btd,ed->bte', x, Wr)
        top_vals, top_idx = jax.lax.top_k(logits, K)
        w = jax.nn.softmax(top_vals, axis=-1)
        flat_e = top_idx.reshape(Bb, Tt * K)
        oh = jax.nn.one_hot(flat_e, Ee, dtype=jnp.int32)
        pos_all = jnp.cumsum(oh, axis=1) - oh
        pos = jnp.take_along_axis(pos_all, flat_e[..., None], axis=-1)[..., 0]
        keep = pos < C
        b_idx = jnp.arange(Bb, dtype=jnp.int32)[:, None]
        dst = (b_idx * Ee + flat_e) * C + pos
        dst = jnp.where(keep, dst, Bb * Ee * C).reshape(-1)
        x_rep = jnp.repeat(x, K, axis=1).reshape(-1, Dd)
        buf = jnp.zeros((Bb * Ee * C, Dd), dtype=x.dtype).at[dst].add(x_rep, mode='drop')
        expert_in = buf.reshape(Bb, Ee, C, Dd)
        expert_out = jnp.einsum('becd,edf->becf', expert_in, We)
        gathered = jnp.take(expert_out.reshape(Bb * Ee * C, Dd), dst, axis=0, mode='fill', fill_value=0.0)
        gathered = gathered.reshape(Bb, Tt, K, Dd)
        out = jnp.einsum('btk,btkd->btd', w, gathered)
        return out
    x = L0_attn_x
    x = x + 0.5 * _L0_ffn_ref(_layernorm(x, axis=-1), L0_ffn_Wr, L0_ffn_We)
    x = x + _L0_attn_ref(_layernorm(x, axis=-1), L0_attn_Wq, L0_attn_bq, L0_attn_Wk, L0_attn_bk, L0_attn_Wv, L0_attn_bv, L0_attn_Wo, L0_attn_bo)
    x = x + 0.5 * _L0_ffn_ref(_layernorm(x, axis=-1), L0_ffn_Wr, L0_ffn_We)
    return x

_drawn_inputs = setup_inputs


def setup_inputs(seed=0):
    import zlib

    import numpy as np

    out = dict(_drawn_inputs(seed))
    spreads = {'L0_attn_bq': (0.0, 0.333),
     'L0_attn_bk': (0.0, 0.8),
     'L0_attn_bv': (0.0, 0.1),
     'L0_attn_bo': (0.0, 0.1)}
    factors = {}
    for name, (base, spread) in spreads.items():
        noise = np.random.default_rng([zlib.crc32(name.encode()), seed]).standard_normal(out[name].shape)
        drawn = base * np.exp(spread * noise) if base else spread * noise
        out[name] = jnp.asarray(drawn.astype(out[name].dtype))
    for name, factor in factors.items():
        out[name] = (out[name] * factor).astype(out[name].dtype)
    return out
```

```python
from contextlib import ExitStack

import numpy as np

import concourse.bass as bass
from concourse import mybir

F32 = mybir.dt.float32
U32 = mybir.dt.uint32
BF16 = mybir.dt.bfloat16
ALU = mybir.AluOpType
ACT = mybir.ActivationFunctionType
AX = mybir.AxisListType

P = 128
NSEQ, S, D = 16, 512, 128
T = S // P
H, HD = 16, 8
E, TOP_K = 8, 2
CAP = int(S * TOP_K / E * 1.5) + 1
EPS = 1e-5
DMA = 16

Q_PARTS = [0, 0, 0, 1, 1, 2]
K_PARTS = [0, 1, 2, 0, 1, 0]
HEAD_ROWS = len(Q_PARTS) * HD
ALIBI_ROW = 2 * HEAD_ROWS
STEP_ROW = ALIBI_ROW + 3
STEP = 32
STEPS = S // STEP - 1
SHIFT_ROW = STEP_ROW + STEPS
MAX_K = SHIFT_ROW
ALL_K = SHIFT_ROW + 2
PAIRS = H // 2
GROUPS = H // 4
VW = 32


def bf16_parts(a, n):
    parts, rest = [], np.asarray(a, np.float64)
    for _ in range(n):
        bits = rest.astype(np.float32).view(np.uint32)
        bits = (bits + 0x7FFF + ((bits >> 16) & 1)) & np.uint32(0xFFFF0000)
        parts.append((bits >> 16).astype(np.uint16))
        rest = rest - bits.view(np.float32).astype(np.float64)
    return parts


def after(b, n):
    return not isinstance(b, int) or b > n


class Consts:

    def __init__(self, nc, ctx):
        i = np.arange(P)
        one = bf16_parts(np.ones(1), 1)[0][0]
        eye = np.eye(P, dtype=np.float32)
        number = np.broadcast_to(np.arange(E).astype(np.float32), (P, E))
        before = (i[:, None] < i[None, :]).astype(np.float64)
        future = np.where(i[None, :] > i[:, None], -1e30, 0.0)
        b16 = np.concatenate([bf16_parts(a, 1)[0] for a in (eye, future, before, np.ones((P, P)))], axis=1)
        f32 = np.ascontiguousarray(np.concatenate([eye, number], axis=1))
        self.loads = []

        def place(name, data, dtype):
            src = nc.inline_tensor(np.ascontiguousarray(data), name + "_const")
            dst = ctx.enter_context(nc.sbuf_tensor(name, list(data.shape), dtype))
            src = src.ap() if dtype == F32 else src.ap().bitcast(dtype)
            self.loads.append((dst, src))
            return dst

        f = place("f32_consts", f32, F32)
        b = place("bf16_consts", b16, BF16)
        self.ident = f[:, 0:P]
        self.number = f[:, P:P + E]
        self.ident_b = b[:, 0:P]
        self.future_b = b[:, P:2 * P]
        self.before_b = b[:, 2 * P:3 * P]
        self.ones_b = b[:, 3 * P:4 * P]

        slopes = (np.float32(2.0 ** (-8.0 / H)) ** np.arange(1, H + 1, dtype=np.float32)).astype(np.float64)
        block = np.arange(S)[None, :] // STEP
        self.k_rows = []
        for ab in range(2):
            rows = np.zeros((ALL_K - ALIBI_ROW, PAIRS, S), np.uint16)
            rows[0:3] = bf16_parts(slopes[ab::2, None] * np.arange(S)[None, :], 3)
            rows[3:3 + STEPS] = bf16_parts(np.where(block == np.arange(1, STEPS + 1)[:, None], -1e30, 0.0), 1)[0][:, None]
            rows[3 + STEPS + ab] = one
            self.k_rows.append(nc.inline_tensor(rows, f"k_rows_{ab}").ap().bitcast(BF16))
        rows = np.full((3 + STEPS, PAIRS, S), one, np.uint16)
        rows[3:] = np.where(block < np.arange(1, STEPS + 1)[:, None], one, 0)[:, None]
        self.q_rows = nc.inline_tensor(rows, "q_rows").ap().bitcast(BF16)


def moe_layer(nc, tag, x, consts, Wr, We, x_in=None, out=None):
    with ExitStack() as ctx:
        def sb(name, shape, dt=F32):
            return ctx.enter_context(nc.sbuf_tensor(f"{tag}_{name}", shape, dt))

        def ps(name, shape):
            return ctx.enter_context(nc.psum_tensor(f"{tag}_{name}", shape, F32))

        def sem(name):
            return ctx.enter_context(nc.semaphore(f"{tag}_{name}"))

        we = sb("we", [P, E, D])
        wrT = sb("wrT", [P, E])
        bn = sb("bn", [P, T, 6])
        mean_var = sb("mean_var", [P, T, 2])
        half_neg = sb("half_neg", [P, T])
        veps = sb("veps", [P, T])
        rstd = sb("rstd", [P, T])
        mr = sb("mr", [P, T])
        nmr = sb("nmr", [P, T])
        hn = sb("hn", [P, T, D])
        hT = [sb(f"hT{i}", [P, S]) for i in range(2)]
        L = sb("L", [P, T, E])
        top = sb("top", [P, T, E])
        top_at = sb("top_at", [P, T, E], U32)
        first = sb("first", [P, T, E])
        second = sb("second", [P, T, E])
        picks = sb("picks", [P, T, E], BF16)
        gap = sb("gap", [P, T])
        egap = sb("egap", [P, T])
        den = sb("den", [P, T])
        w1 = sb("w1", [P, T])
        g2 = sb("g2", [P, T, E])
        g12 = sb("g12", [P, T, E])
        gw = sb("gw", [P, T, E])
        gates = [sb(f"gates{i}", [P, T, E]) for i in range(2)]
        HE = E // 2
        scaled = [sb(f"scaled{i}", [P, HE, D]) for i in range(2)]
        part2 = sb("part2", [P, 2, D])
        part1 = sb("part1", [P, D])

        lo_ps = [ps(f"lo{t}", [P, HE, D]) for t in range(T)]
        hi_ps = [ps(f"hi{t}", [P, HE, D]) for t in range(2)]
        hT_ps = ps("hT_ps", [P, S])
        route_ps = ps("route_ps", [P, 2, T, E])

        w_in = sem("w_in")
        x_loaded = [sem("x_loaded0"), sem("x_loaded1")]
        bn_done = sem("bn_done")
        stats_done = sem("stats_done")
        dve_passed, pool_passed = sem("dve_passed"), sem("pool_passed")
        half_set = sem("half_set")
        rstd_step = sem("rstd_step")
        RS = 4
        hn_done = sem("hn_done")
        hT_out = sem("hT_out")
        hT_copied = sem("hT_copied")
        logits_out = sem("logits_out")
        places_out = sem("places_out")
        route_step = sem("route_step")
        RT, GAP, PICKED = 12, 4, 7
        egap_done = sem("egap_done")
        lo_out, hi_out = sem("lo_out"), sem("hi_out")
        acc_step = sem("acc_step")
        scaled_done = sem("scaled_done")
        part_step = sem("part_step")
        stored = sem("stored")

        block = ctx.enter_context(nc.Block())

        def xt(b, t):
            return x[:, bass.ds((b * T + t) * D, D)]

        def sequence(b):
            return x[:, bass.ds(b * (T * D), T * D)].rearrange("p (t d) -> p t d", d=D)

        def added(b, t, e):
            n = b * T + t
            if isinstance(n, int) and n == 0 and e < 2:
                return e + 1
            if isinstance(n, int) and n == NSEQ * T - 1 and e >= 2:
                return n * HE + e + 1
            return n * HE + (-1, 1, 4, 6)[e]

        def all_steps(eng, step):
            step(-1, 1, 0, False, True, True)
            step(0, 0, 1, True, True, True)
            with eng.Fori(0, NSEQ // 2 - 2) as i:
                step(2 * i + 1, 1, i + 1, True, True, True)
                step(2 * i + 2, 0, i + 2, True, True, True)
            step(NSEQ - 3, 1, NSEQ // 2 - 1, True, True, True)
            step(NSEQ - 2, 0, NSEQ // 2, True, True, False)
            step(NSEQ - 1, 1, NSEQ // 2, True, False, False)

        @block.sync
        def _(sp):
            sp.dma_start(we[:], We.rearrange("e d f -> d e f")).then_inc(w_in, DMA)
            with nc.allow_non_contiguous_dma(reason="the router's 1024 weights, once"):
                sp.dma_start(wrT[:], Wr.rearrange("e d -> d e")).then_inc(w_in, DMA)
            if x_in is not None:
                src = x_in.rearrange("b (t p) d -> p (b t) d", p=P)

                def load(b, u):
                    sp.dma_start(sequence(b), src[:, bass.ds(b * T, T), :]).then_inc(x_loaded[u], DMA)

                load(0, 0)
                load(1, 1)
                with sp.Fori(1, NSEQ // 2) as i:
                    for u in range(2):
                        sp.wait_ge(x_loaded[u], i * DMA)
                        load(2 * i + u, u)
            if out is not None:
                dst = out.rearrange("b (t p) d -> p (b t) d", p=P)
                with sp.Fori(0, NSEQ) as b:
                    sp.wait_ge(part_step, b * (3 * T) + 3 * T)
                    sp.dma_start(dst[:, bass.ds(b * T, T), :], sequence(b)).then_inc(stored, DMA)
                sp.wait_ge(stored, NSEQ * DMA)

        @block.tensor
        def _(pe):
            def turn_h(b, par):
                pe.wait_ge(hn_done, b + 1)
                if after(b, 0):
                    pe.wait_ge(hT_copied, b)
                for t in range(T):
                    mm = nc.tensor.transpose(hT_ps[:, t * P:(t + 1) * P], hn[:, t, :], consts.ident)
                mm.then_inc(hT_out, 1)

            def logits(b, par):
                pe.wait_ge(hT_copied, b + 1)
                if after(b, 0):
                    pe.wait_ge(route_step, b * RT)
                for t in range(T):
                    mm = nc.tensor.matmul(route_ps[:, 0, t, :], hT[par][:, t * P:(t + 1) * P], wrT[:],
                                          start=True, stop=True)
                mm.then_inc(logits_out, 1)

            def places(b):
                pe.wait_ge(route_step, b * RT + PICKED)
                nc.tensor.matmul(route_ps[:, 1, :, :], consts.before_b, picks[:], start=True, stop=False)
                for s in range(1, T):
                    mm = nc.tensor.matmul(route_ps[:, 1, s:T, :], consts.ones_b, picks[:, 0:T - s, :],
                                          start=False, stop=(s == T - 1))
                mm.then_inc(places_out, 1)

            def experts(b, par, t):
                if after(b, 0):
                    pe.wait_ge(acc_step, added(b - 1, t, HE - 1))
                nc.tensor.matmul(lo_ps[t][:], hT[par][:, t * P:(t + 1) * P], we[:, 0:HE, :],
                                 start=True, stop=True).then_inc(lo_out, 1)
                if after(b, 0) or t >= 2:
                    pe.wait_ge(scaled_done, b * T + t - 1)
                nc.tensor.matmul(hi_ps[t % 2][:], hT[par][:, t * P:(t + 1) * P], we[:, HE:E, :],
                                 start=True, stop=True).then_inc(hi_out, 1)

            def step(b, par, half, this, next1, next2):
                if next1:
                    turn_h(b + 1, 1 - par)
                if this:
                    experts(b, par, 0)
                if next1:
                    logits(b + 1, 1 - par)
                if this:
                    experts(b, par, 1)
                    experts(b, par, 2)
                if next1:
                    places(b + 1)
                if this:
                    experts(b, par, 3)

            pe.wait_ge(w_in, 2 * DMA)
            all_steps(pe, step)

        @block.scalar
        def _(act):
            def normalise(b, par):
                act.wait_ge(rstd_step, b * RS + RS)
                if after(b, 0):
                    act.wait_ge(hT_out, b)
                for t in range(T):
                    ins = nc.scalar.activation(hn[:, t, :], xt(b, t), ACT.Identity,
                                               bias=nmr[:, t:t + 1], scale=rstd[:, t:t + 1])
                ins.then_inc(hn_done, 1)

            def copy_hT(b, par):
                act.wait_ge(hT_out, b + 1)
                if after(b, 1):
                    act.wait_ge(hi_out, (b - 1) * T)
                nc.scalar.activation(hT[par][:], hT_ps[:], ACT.Copy).then_inc(hT_copied, 1)

            def exp_gap(b):
                act.wait_ge(route_step, b * RT + GAP)
                nc.scalar.activation(egap[:], gap[:], ACT.Exp).then_inc(egap_done, 1)

            def scale_products(b, par, t):
                act.wait_ge(hi_out, b * T + t + 1)
                if after(b, 0) or t >= 2:
                    act.wait_ge(part_step, (b * T + t - 1) * 3)
                if t == 0:
                    act.wait_ge(route_step, b * RT + RT)
                for e in range(HE):
                    ins = nc.scalar.activation(scaled[t % 2][:, e, :], hi_ps[t % 2][:, e, :], ACT.Copy,
                                               scale=gates[par][:, t, HE + e:HE + e + 1])
                ins.then_inc(scaled_done, 1)

            def step(b, par, half, this, next1, next2):
                if next1:
                    copy_hT(b + 1, 1 - par)
                if this:
                    scale_products(b, par, 0)
                    scale_products(b, par, 1)
                if next2:
                    normalise(b + 2, par)
                if this:
                    scale_products(b, par, 2)
                if next1:
                    exp_gap(b + 1)
                if this:
                    scale_products(b, par, 3)

            normalise(0, 0)
            all_steps(act, step)

        @block.gpsimd
        def _(pool):
            def inverse_spread(b, par):
                pool.wait_ge(stats_done, b + 1)
                if after(b, 0):
                    pool.wait_ge(hn_done, b)
                pool.sem_inc(pool_passed, 1)
                nc.gpsimd.tensor_scalar(veps[:], mean_var[:, :, 1], 1.0, EPS, ALU.mult, ALU.add).then_inc(rstd_step, 1)
                pool.wait_ge(rstd_step, b * RS + 1)
                nc.gpsimd.tensor_tensor(rstd[:], veps[:], half_neg[:], ALU.pow).then_inc(rstd_step, 1)
                pool.wait_ge(rstd_step, b * RS + 2)
                nc.gpsimd.tensor_tensor(mr[:], mean_var[:, :, 0], rstd[:], ALU.mult).then_inc(rstd_step, 1)
                pool.wait_ge(rstd_step, b * RS + 3)
                pool.sem_inc(pool_passed, 1)
                nc.gpsimd.tensor_scalar(nmr[:], mr[:], -1.0, 0.0, ALU.mult, ALU.add).then_inc(rstd_step, 1)

            def add_parts(b, par, t):
                n = b * T + t
                pool.wait_ge(scaled_done, n + 1)
                nc.gpsimd.tensor_tensor(part2[:], scaled[t % 2][:, 0:2, :], scaled[t % 2][:, 2:4, :],
                                        ALU.add).then_inc(part_step, 1)
                pool.wait_ge(part_step, n * 3 + 1)
                nc.gpsimd.tensor_tensor(part1[:], part2[:, 0, :], part2[:, 1, :], ALU.add).then_inc(part_step, 1)
                pool.wait_ge(part_step, n * 3 + 2)
                pool.wait_ge(acc_step, added(b, t, HE - 1))
                nc.gpsimd.tensor_tensor(xt(b, t), xt(b, t), part1[:], ALU.add).then_inc(part_step, 1)

            def step(b, par, half, this, next1, next2):
                if next2:
                    inverse_spread(b + 2, par)
                if this:
                    for t in range(T):
                        add_parts(b, par, t)

            nc.gpsimd.memset(half_neg[:], -0.5).then_inc(half_set, 1)
            pool.wait_ge(half_set, 1)
            inverse_spread(0, 0)
            all_steps(pool, step)

        @block.vector
        def _(dve):
            def statistics(b, par, half):
                if x_in is not None:
                    dve.wait_ge(x_loaded[par], half * DMA + DMA)
                if after(b, 0):
                    dve.wait_ge(rstd_step, b * RS)
                for t in range(T):
                    ins = nc.vector.bn_stats(bn[:, t, :], xt(b, t))
                ins.then_inc(bn_done, 1)

            def aggregate(b):
                dve.wait_ge(bn_done, b + 1)
                dve.sem_inc(dve_passed, 1)
                for t in range(T):
                    ins = nc.vector.bn_aggr(mean_var[:, t, :], bn[:, t, :])
                ins.then_inc(stats_done, 1)

            def over_e(a):
                return a.to_broadcast([P, T, E])

            number = consts.number.unsqueeze(1).to_broadcast([P, T, E])

            def route(b, par, n):
                done = b * RT
                if n == 0:
                    dve.wait_ge(logits_out, b + 1)
                    nc.vector.tensor_copy(L[:], route_ps[:, 0]).then_inc(route_step, 1)
                elif n == 1:
                    dve.wait_ge(route_step, done + 1)
                    dve.sem_inc(dve_passed, 1)
                    for t in range(T):
                        ins = nc.vector.max(top[:, t, :], L[:, t, :])
                    ins.then_inc(route_step, 1)
                elif n == 2:
                    dve.wait_ge(route_step, done + 2)
                    dve.sem_inc(dve_passed, 1)
                    for t in range(T):
                        ins = nc.vector.max_index(top_at[:, t, :], top[:, t, :], L[:, t, :])
                    ins.then_inc(route_step, 1)
                    nc.vector.tensor_tensor(gap[:], top[:, :, 1], top[:, :, 0], ALU.subtract).then_inc(
                        route_step, 1)
                elif n == 3:
                    dve.wait_ge(route_step, done + 3)
                    nc.vector.tensor_tensor(first[:], number, over_e(top_at[:, :, 0:1]), ALU.is_equal).then_inc(
                        route_step, 1)
                    nc.vector.tensor_tensor(second[:], number, over_e(top_at[:, :, 1:2]), ALU.is_equal).then_inc(
                        route_step, 1)
                elif n == 4:
                    dve.wait_ge(route_step, done + 6)
                    nc.vector.tensor_tensor(picks[:], first[:], second[:], ALU.add).then_inc(route_step, 1)
                elif n == 5:
                    dve.wait_ge(egap_done, b + 1)
                    nc.vector.tensor_scalar(den[:], egap[:], 1.0, 2.0, ALU.add, ALU.mult).then_inc(route_step, 1)
                    nc.vector.tensor_tensor(g2[:], second[:], over_e(egap[:].unsqueeze(2)), ALU.mult).then_inc(
                        route_step, 1)
                elif n == 6:
                    dve.wait_ge(route_step, done + 9)
                    nc.vector.reciprocal(w1[:], den[:])
                    nc.vector.tensor_tensor(g12[:], g2[:], first[:], ALU.add).then_inc(route_step, 1)
                elif n == 7:
                    dve.wait_ge(route_step, done + 10)
                    nc.vector.tensor_tensor(gw[:], g12[:], over_e(w1[:].unsqueeze(2)), ALU.mult).then_inc(
                        route_step, 1)
                elif n == 8:
                    dve.wait_ge(route_step, done + 11)
                    dve.wait_ge(places_out, b + 1)
                    if after(b, 1):
                        dve.wait_ge(scaled_done, (b - 1) * T)
                    nc.vector.scalar_tensor_tensor(out=gates[par][:], in0=route_ps[:, 1], scalar=float(CAP),
                                                   in1=gw[:], op0=ALU.is_lt, op1=ALU.mult).then_inc(
                        route_step, 1)

            def add_expert(b, par, t, e):
                if e > 0:
                    dve.wait_ge(acc_step, added(b, t, e - 1))
                nc.vector.scalar_tensor_tensor(out=xt(b, t), in0=lo_ps[t][:, e, :],
                                               scalar=gates[par][:, t, e:e + 1], in1=xt(b, t),
                                               op0=ALU.mult, op1=ALU.add).then_inc(acc_step, 1)

            ROUTE_AFTER = {(1, 0): [0], (1, 1): [1], (1, 2): [2], (1, 3): [3], (2, 0): [4], (2, 2): [5],
                           (2, 3): [6], (3, 0): [7], (3, 3): [8]}

            def step(b, par, half, this, next1, next2):
                for t in range(T):
                    if this:
                        dve.wait_ge(lo_out, b * T + t + 1)
                        if t == 0:
                            dve.wait_ge(route_step, b * RT + RT)
                            dve.wait_ge(hn_done, b + 1)
                    for k in range(HE):
                        if this and k % 2 == 0:
                            add_expert(b, par, t, k // 2)
                        elif this and t > 0:
                            add_expert(b, par, t - 1, 2 + k // 2)
                        elif this and after(b, 0):
                            add_expert(b - 1, 1 - par, T - 1, 2 + k // 2)
                        if next1:
                            for n in ROUTE_AFTER.get((t, k), []):
                                route(b + 1, 1 - par, n)
                        if next2 and (t, k) == (0, 1):
                            statistics(b + 2, par, half)
                        if next2 and (t, k) == (0, 3):
                            aggregate(b + 2)

            statistics(0, 0, 0)
            aggregate(0)
            all_steps(dve, step)
            for e in (2, 3):
                add_expert(NSEQ - 1, 1, T - 1, e)


SIDE_WORK = [
    {2: "shift_hi", 5: "turn_o2"},
    {0: "turn_h", 3: "project_q", 5: "turn_o3", 7: "project_k"},
    {0: "turn_o", 3: "shift_lo", 5: "turn_o0", 7: "project_v"},
    {0: "output", 5: "turn_o1"},
]
LN_WORK = {(0, 1): "statistics", (0, 3): "spread", (0, 9): "normalise", (1, 4): "add_bias"}
PV_AFTER = {2: 0, 4: 1, 6: 2, 8: 3}
MAX_UNITS = 11
EXP_UNITS = 10


def max_unit(n):
    return [(0, [0, 1, 2, 3]), (1, [0, 1]), (1, [2, 3]),
            (2, [0]), (2, [1]), (2, [2]), (2, [3]), (3, [0]), (3, [1]), (3, [2]), (3, [3])][n]


def exp_unit(n):
    pair, u = divmod(n, 5)
    return pair, [[(0, 0, 0)], [(0, 1, 0), (0, 3, 3 * P)], [(0, 2, 0), (1, 2, 2 * P)],
                  [(1, 0, 0)], [(1, 1, 0), (1, 3, 3 * P)]][u]


def attention(nc, x, consts, Wq, bq, Wk, bk, Wv, bv, Wo, bo):
    scratch = nc.dram_tensor("qk_parts", [2, 2, 3, P, S], BF16, kind="Internal").ap()
    with ExitStack() as ctx:
        def sb(name, shape, dt=F32):
            return ctx.enter_context(nc.sbuf_tensor(f"att_{name}", shape, dt))

        def ps(name, shape):
            return ctx.enter_context(nc.psum_tensor(f"att_{name}", shape, F32))

        def sem(name):
            return ctx.enter_context(nc.semaphore(f"att_{name}"))

        def both(f):
            return [f(0), f(1)]

        w = {n: sb(n, [P, D]) for n in ("wq", "wk", "wv", "wo")}
        bq_col, bk_col, bq_scaled = sb("bq_col", [P, 1]), sb("bk_col", [P, 1]), sb("bq_scaled", [P, 1])
        bv_rows, bo_rows = sb("bv_rows", [P, D]), sb("bo_rows", [P, D])
        half_neg = sb("half_neg", [P, T])
        bn = sb("bn", [P, T, 6])
        mean_var = sb("mean_var", [P, T, 2])
        veps, rstd, mr, nmr = (sb(n, [P, T]) for n in ("veps", "rstd", "mr", "nmr"))
        hn = sb("hn", [P, T, D])
        hT = both(lambda i: sb(f"hT{i}", [P, S]))
        qk = both(lambda i: sb(f"qk{i}", [P, S]))
        rest = both(lambda i: sb(f"rest{i}", [P, S]))
        parts = both(lambda i: sb(f"parts{i}", [P, 3, S], BF16))
        q_st = both(lambda i: sb(f"q_st{i}", [P, PAIRS, S], BF16))
        k_st = both(lambda i: both(lambda ab: sb(f"k_st{i}{ab}", [P, PAIRS, S], BF16)))
        v = both(lambda i: sb(f"v{i}", [P, T, H, VW]))
        neg_max = both(lambda i: sb(f"neg_max{i}", [P, 2, T, H // 2], BF16))
        shift = sb("shift", [T * H // 2, P], BF16)
        probs = both(lambda i: sb(f"probs{i}", [P, EXP_UNITS, S]))
        oT = sb("oT", [P, S])
        rden = sb("rden", [P, T, 4])
        o = sb("o", [P, T, D])
        o_fm = sb("o_fm", [P, S])

        RING = 3
        max_ps = [ps(f"max{i}", [P, S]) for i in range(RING)]
        exp_ps = [ps(f"exp{i}", [P, S]) for i in range(RING)]
        pv_ps = ps("pv", [P, S])
        side_ps = ps("side", [P, S])

        w_in, rows_in, zeroed = sem("w_in"), sem("rows_in"), sem("zeroed")
        bias_scaled, v_set = sem("bias_scaled"), sem("v_set")
        pool_passed, dve_passed = sem("pool_passed"), sem("dve_passed")
        half_set = sem("half_set")
        bn_done, stats_done, rstd_step = sem("bn_done"), sem("stats_done"), sem("rstd_step")
        RS = 4
        hn_done = sem("hn_done")
        bias_added = sem("bias_added")
        split_step = sem("split_step")
        scratch_in = both(lambda i: both(lambda s: sem(f"scratch_in{i}{s}")))
        stack_in = both(lambda i: both(lambda hf: sem(f"stack_in{i}{hf}")))
        shift_in = both(lambda i: both(lambda hf: sem(f"shift_in{i}{hf}")))
        STACK_DMAS = 2 * 2 * len(Q_PARTS)
        max_out = sem("max_out")
        max_read = sem("max_read")
        exp_out = sem("exp_out")
        exp_done = sem("exp_done")
        masked = sem("masked")
        pv_out = sem("pv_out")
        pv_read = sem("pv_read")
        turned = sem("turned")
        side_read = sem("side_read")
        rden_done = sem("rden_done")
        NM, NE = GROUPS * MAX_UNITS, GROUPS * EXP_UNITS

        order = [what for g in SIDE_WORK for what in g.values()]

        def present(b, what):
            if not isinstance(b, int):
                return True
            offset = {"turn_h": 2, "project_q": 2, "project_k": 2, "project_v": 1, "shift_lo": 1, "shift_hi": 0,
                      "turn_o2": -1, "turn_o3": -1, "turn_o": -1, "output": -1, "turn_o0": 0, "turn_o1": 0}[what]
            return 0 <= b + offset < NSEQ

        L = len(order)
        before = {-2: 0}
        for n in range(-1, 3):
            before[n] = before[n - 1] + sum(present(n - 1, what) for what in order)
        before[NSEQ - 2] = before[2] + (NSEQ - 4) * L
        for n in range(NSEQ - 1, NSEQ + 2):
            before[n] = before[n - 1] + sum(present(n - 1, what) for what in order)

        def use(b, what):
            here = order[:order.index(what) + 1]
            if isinstance(b, int) and b in before:
                return before[b] + sum(present(b, w) for w in here)
            return b * L + (before[2] - 2 * L + len(here))

        block = ctx.enter_context(nc.Block())

        def xt(b, t):
            return x[:, bass.ds((b * T + t) * D, D)]

        def sequence(b):
            return x[:, bass.ds(b * (T * D), T * D)].rearrange("p (t d) -> p t d", d=D)

        def all_steps(eng, step):
            for b in range(-2, 2):
                step(b, b % 2, b // 2)
            with eng.Fori(1, NSEQ // 2 - 1) as i:
                step(2 * i, 0, i)
                step(2 * i + 1, 1, i)
            for b in range(NSEQ - 2, NSEQ + 1):
                step(b, b % 2, b // 2)

        def there(b):
            return not isinstance(b, int) or 0 <= b < NSEQ

        def walk(b, par, half, on_max=None, on_exp=None, on_pv=None, on_side=None, on_ln=None):
            for g in range(GROUPS):
                for n in range(MAX_UNITS):
                    if on_max and there(b + 1):
                        on_max(b + 1, 1 - par, half + par, g, n)
                    if on_exp and n < EXP_UNITS and there(b):
                        on_exp(b, par, half, g, n)
                    if on_ln and (g, n) in LN_WORK and there(b + 2):
                        on_ln(b + 2, par, half + 1, LN_WORK[g, n])
                    if on_side and n in SIDE_WORK[g] and present(b, SIDE_WORK[g][n]):
                        on_side(b, par, half, SIDE_WORK[g][n])
                    if on_pv and n in PV_AFTER:
                        if g > 0 and there(b):
                            on_pv(b, par, g - 1, PV_AFTER[n])
                        if g == 0 and there(b - 1):
                            on_pv(b - 1, 1 - par, GROUPS - 1, PV_AFTER[n])

        @block.sync
        def _(sp):
            for n, W in (("wq", Wq), ("wk", Wk), ("wv", Wv), ("wo", Wo)):
                sp.dma_start(w[n][:], W).then_inc(w_in, DMA)
            sp.dma_start(bq_col[:], bq.rearrange("(p a) -> p a", a=1)).then_inc(w_in, DMA)
            sp.dma_start(bk_col[:], bk.rearrange("(p a) -> p a", a=1)).then_inc(w_in, DMA)
            sp.dma_start(bv_rows[:], bv.partition_broadcast(P)).then_inc(w_in, DMA)
            sp.dma_start(bo_rows[:], bo.partition_broadcast(P)).then_inc(w_in, DMA)
            sp.wait_ge(zeroed, 4)
            for i in range(2):
                sp.dma_start(q_st[i][ALIBI_ROW:SHIFT_ROW], consts.q_rows).then_inc(rows_in, DMA)
                for ab in range(2):
                    sp.dma_start(k_st[i][ab][ALIBI_ROW:ALL_K], consts.k_rows[ab]).then_inc(rows_in, DMA)

            def store_parts(b, par, half, side):
                sp.wait_ge(split_step, b * 8 + 4 * side + 4)
                sp.dma_start(scratch[par, side].rearrange("c p s -> p c s"), parts[side][:]).then_inc(
                    scratch_in[par][side], DMA)

            def stack(b, par, half, hf):
                if hf == 0:
                    for side in range(2):
                        sp.wait_ge(scratch_in[par][side], half * DMA + DMA)
                if after(b, 1):
                    sp.wait_ge(exp_out, (b - 2) * NE + (hf + 1) * NE // 2)
                pairs = slice(hf * PAIRS // 2, (hf + 1) * PAIRS // 2)
                for side, which in ((0, Q_PARTS), (1, K_PARTS)):
                    for ab in range(2):
                        for term, part in enumerate(which):
                            dst = q_st[par] if side == 0 else k_st[par][ab]
                            row = ab * HEAD_ROWS + term * HD
                            src = scratch[par, side, part].rearrange("(r u d) s -> u d r s", u=2, d=HD)
                            sp.dma_start(dst[row:row + HD, pairs, :], src[ab, :, pairs, :]).then_inc(
                                stack_in[par][hf], DMA)

            def place_shift(b, par, half, hf):
                sp.wait_ge(side_read, use(b if hf else b - 1, "shift_hi" if hf else "shift_lo"))
                pairs = slice(hf * PAIRS // 2, (hf + 1) * PAIRS // 2)
                for ab in range(2):
                    for t in range(T):
                        src = shift[t * H // 2 + ab:(t + 1) * H // 2:2, :]
                        dst = q_st[par][SHIFT_ROW + ab:SHIFT_ROW + ab + 1, pairs, t * P:(t + 1) * P]
                        sp.dma_start(dst, src).then_inc(shift_in[par][hf], DMA)

            def step(b, par, half):
                if there(b):
                    place_shift(b, par, half, 1)
                if there(b + 2):
                    store_parts(b + 2, par, half + 1, 0)
                    store_parts(b + 2, par, half + 1, 1)
                    stack(b + 2, par, half + 1, 0)
                if there(b + 1):
                    place_shift(b + 1, 1 - par, half, 0)
                if there(b + 2):
                    stack(b + 2, par, half + 1, 1)

            all_steps(sp, step)

        @block.tensor
        def _(pe):
            def take_max_scores(b, par, half, g, n):
                i, heads = max_unit(n)
                m = g * MAX_UNITS + n
                if n == 0 and g in (0, 2):
                    pe.wait_ge(stack_in[par][g // 2], half * (STACK_DMAS * DMA) + STACK_DMAS * DMA)
                if m >= RING:
                    pe.wait_ge(max_read, b * NM + (m - RING + 1))
                elif after(b, 0):
                    last = max(k for k in range(NM) if k % RING == m % RING)
                    pe.wait_ge(max_read, (b - 1) * NM + (last + 1))
                width = (i + 1) * P
                for c, hh in enumerate(heads):
                    r, ab = divmod(4 * g + hh, 2)
                    nc.tensor.matmul(max_ps[m % RING][:, c * width:(c + 1) * width],
                                     q_st[par][0:MAX_K, r, i * P:(i + 1) * P], k_st[par][ab][0:MAX_K, r, 0:width],
                                     start=True, stop=False)
                    mm = nc.tensor.matmul(max_ps[m % RING][:, (c + 1) * width - P:(c + 1) * width],
                                          consts.ident_b, consts.future_b, start=False, stop=True)
                mm.then_inc(max_out, 1)

            def take_exp_scores(b, par, half, g, n):
                pair, pieces = exp_unit(n)
                m = g * EXP_UNITS + n
                if n == 0 and g in (0, 2):
                    pe.wait_ge(shift_in[par][g // 2], half * (2 * T * DMA) + 2 * T * DMA)
                if m >= RING:
                    pe.wait_ge(exp_done, b * NE + (m - RING + 1))
                elif after(b, 0):
                    last = max(k for k in range(NE) if k % RING == m % RING)
                    pe.wait_ge(exp_done, (b - 1) * NE + (last + 1))
                r = 2 * g + pair
                for ab, j, c in pieces:
                    mm = nc.tensor.matmul(exp_ps[m % RING][:, c:c + S - j * P],
                                          k_st[par][ab][0:ALL_K, r, j * P:(j + 1) * P],
                                          q_st[par][0:ALL_K, r, j * P:S], start=True, stop=True)
                mm.then_inc(exp_out, 1)

            def weigh_values(b, par, g, j):
                if j == 0:
                    pe.wait_ge(masked, b * NE + (g + 1) * EXP_UNITS)
                    if g > 0 or after(b, 0):
                        pe.wait_ge(pv_read, b * GROUPS + g)
                    if g == 0:
                        pe.wait_ge(side_read, use(b - 1, "project_v"))
                for hh in range(4):
                    pair, ab = divmod(hh, 2)
                    n, c = next((n, c) for n in range(EXP_UNITS) for a, jj, c in exp_unit(n)[1]
                                if exp_unit(n)[0] == pair and (a, jj) == (ab, j))
                    mm = nc.tensor.matmul(pv_ps[VW * hh:VW * (hh + 1), j * P:S], v[par][:, j, 4 * g + hh, :],
                                          probs[g % 2][:, n, c:c + S - j * P], start=(j == 0), stop=(j == T - 1))
                if j == T - 1:
                    mm.then_inc(pv_out, 1)

            def side(b, par, half, what):
                n = use(b, what)
                if not isinstance(n, int) or n > 1:
                    pe.wait_ge(side_read, n - 1)
                if what == "turn_h":
                    pe.wait_ge(hn_done, b + 3)
                    for t in range(T):
                        mm = nc.tensor.transpose(side_ps[:, t * P:(t + 1) * P], hn[:, t, :], consts.ident)
                elif what in ("project_q", "project_k"):
                    mm = nc.tensor.matmul(side_ps[:], w["wq" if what == "project_q" else "wk"][:], hT[par][:],
                                          start=True, stop=True)
                elif what == "project_v":
                    for t in range(T):
                        mm = nc.tensor.matmul(side_ps[:, t * P:(t + 1) * P], hT[1 - par][:, t * P:(t + 1) * P],
                                              w["wv"][:], start=True, stop=True)
                elif what in ("shift_lo", "shift_hi"):
                    hi = what == "shift_hi"
                    pe.wait_ge(max_read, (b if hi else b + 1) * NM + (NM if hi else NM // 2))
                    mm = nc.tensor.transpose(side_ps[0:T * H // 2, 0:P // 2].bitcast(BF16),
                                             neg_max[par if hi else 1 - par][:, int(hi)], consts.ident_b)
                elif what == "turn_o":
                    pe.wait_ge(side_read, use(b, "turn_o3"))
                    for t in range(T):
                        mm = nc.tensor.transpose(side_ps[:, t * P:(t + 1) * P], o[:, t, :], consts.ident)
                elif what == "output":
                    for t in range(T):
                        mm = nc.tensor.matmul(side_ps[:, t * P:(t + 1) * P], o_fm[:, t * P:(t + 1) * P],
                                              w["wo"][:], start=True, stop=True)
                else:
                    g = int(what[-1])
                    pe.wait_ge(pv_read, (b - 1 if g >= 2 else b) * GROUPS + (g + 1))
                    for t in range(T):
                        mm = nc.tensor.transpose(side_ps[:, t * P:(t + 1) * P], oT[:, t * P:(t + 1) * P], consts.ident)
                mm.then_inc(turned, 1)

            def step(b, par, half):
                walk(b, par, half, take_max_scores, take_exp_scores, weigh_values, side)

            pe.wait_ge(w_in, 8 * DMA)
            pe.wait_ge(rows_in, 6 * DMA)
            all_steps(pe, step)

        @block.scalar
        def _(act):
            def exponentiate(b, par, half, g, n):
                m = g * EXP_UNITS + n
                act.wait_ge(exp_out, b * NE + (m + 1))
                if n == 0:
                    if g >= 2:
                        act.wait_ge(pv_out, b * GROUPS + (g - 1))
                    elif after(b, 0):
                        act.wait_ge(pv_out, (b - 1) * GROUPS + (g + 3))
                nc.scalar.activation(probs[g % 2][:, n, :], exp_ps[m % RING][:], ACT.Exp).then_inc(exp_done, 1)

            def copy_values(b, par, g, j):
                if j < T - 1:
                    return
                act.wait_ge(pv_out, b * GROUPS + (g + 1))
                if g > 0 or after(b, 0):
                    act.wait_ge(turned, use(b + 1 if g == 3 else b, f"turn_o{(g - 1) % GROUPS}"))
                nc.scalar.activation(oT[:], pv_ps[:], ACT.Copy).then_inc(pv_read, 1)

            def side(b, par, half, what):
                if what in ("project_v", "output") or what[:-1] == "turn_o":
                    return
                act.wait_ge(turned, use(b, what))
                if what == "turn_h":
                    nc.scalar.activation(hT[par][:], side_ps[:], ACT.Copy).then_inc(side_read, 1)
                elif what in ("project_q", "project_k"):
                    s = int(what == "project_k")
                    if after(b, -2):
                        act.wait_ge(split_step, (b + 1) * 8 + 4 * s + 4)
                    nc.scalar.activation(qk[s][:], side_ps[:], ACT.Identity,
                                         bias=(bk_col if s else bq_scaled)[:],
                                         scale=1.0 if s else HD ** -0.5).then_inc(side_read, 1)
                elif what in ("shift_lo", "shift_hi"):
                    hi = what == "shift_hi"
                    if hi:
                        act.wait_ge(shift_in[par][0], (half + 1) * (2 * T * DMA))
                    elif after(b, -1):
                        act.wait_ge(shift_in[par][1], (half + 1) * (2 * T * DMA))
                    nc.scalar.activation(shift[:], side_ps[0:T * H // 2, 0:P // 2].bitcast(BF16),
                                         ACT.Copy).then_inc(side_read, 1)
                elif what == "turn_o":
                    nc.scalar.activation(o_fm[:], side_ps[:], ACT.Copy).then_inc(side_read, 1)

            def normalise(b, par, half, what):
                if what != "normalise":
                    return
                act.wait_ge(rstd_step, b * RS + RS)
                if after(b, 0):
                    act.wait_ge(turned, use(b - 3, "turn_h"))
                for t in range(T):
                    ins = nc.scalar.activation(hn[:, t, :], xt(b, t), ACT.Identity,
                                               bias=nmr[:, t:t + 1], scale=rstd[:, t:t + 1])
                ins.then_inc(hn_done, 1)

            def step(b, par, half):
                walk(b, par, half, None, exponentiate, copy_values, side, normalise)

            act.wait_ge(w_in, 8 * DMA)
            nc.scalar.activation(bq_scaled[:], bq_col[:], ACT.Copy, scale=HD ** -0.5).then_inc(bias_scaled, 1)
            act.wait_ge(bias_scaled, 1)
            all_steps(act, step)

        @block.gpsimd
        def _(pool):
            def mask(b, par, half, g, n):
                pieces = exp_unit(n)[1]
                view = probs[g % 2][:, n, :].rearrange("p (a c) -> p a c", c=P)
                blocks = [c // P for _, _, c in pieces]
                view = view[:, 0:1, :] if len(blocks) == 1 else view[:, 0:blocks[1] + 1:blocks[1], :]
                pool.wait_ge(exp_done, b * NE + (g * EXP_UNITS + n + 1))
                pool.sem_inc(pool_passed, 1)
                nc.gpsimd.affine_select(out=view, in_=view, compare_op=ALU.is_ge, fill=0.0, base=0,
                                        pattern=[[0, len(blocks)], [1, P]], channel_multiplier=-1).then_inc(masked, 1)

            def split(b, par, half, what):
                if what not in ("project_q", "project_k"):
                    return
                s = int(what == "project_k")
                first = (b + 2) * 8 + 4 * s
                pool.wait_ge(side_read, use(b, what))
                if after(b, -2):
                    pool.wait_ge(scratch_in[1 - par][s], (half + par) * DMA + DMA)
                pool.sem_inc(pool_passed, 1)
                nc.gpsimd.tensor_scalar(parts[s][:, 0], qk[s][:], 1.0, 1.0, ALU.mult, ALU.mult).then_inc(split_step, 1)
                pool.wait_ge(split_step, first + 1)
                nc.gpsimd.tensor_tensor(rest[s][:], qk[s][:], parts[s][:, 0], ALU.subtract).then_inc(split_step, 1)
                pool.wait_ge(split_step, first + 2)
                pool.sem_inc(pool_passed, 1)
                nc.gpsimd.tensor_scalar(parts[s][:, 1], rest[s][:], 1.0, 1.0, ALU.mult, ALU.mult).then_inc(split_step, 1)
                pool.wait_ge(split_step, first + 3)
                nc.gpsimd.tensor_tensor(parts[s][:, 2], rest[s][:], parts[s][:, 1], ALU.subtract).then_inc(split_step, 1)

            def spread(b, par, half, what):
                if what == "spread":
                    pool.wait_ge(stats_done, b + 1)
                    if after(b, 0):
                        pool.wait_ge(hn_done, b)
                    pool.sem_inc(pool_passed, 1)
                    nc.gpsimd.tensor_scalar(veps[:], mean_var[:, :, 1], 1.0, EPS, ALU.mult, ALU.add).then_inc(
                        rstd_step, 1)
                    pool.wait_ge(rstd_step, b * RS + 1)
                    nc.gpsimd.tensor_tensor(rstd[:], veps[:], half_neg[:], ALU.pow).then_inc(rstd_step, 1)
                    pool.wait_ge(rstd_step, b * RS + 2)
                    nc.gpsimd.tensor_tensor(mr[:], mean_var[:, :, 0], rstd[:], ALU.mult).then_inc(rstd_step, 1)
                    pool.wait_ge(rstd_step, b * RS + 3)
                    pool.sem_inc(pool_passed, 1)
                    nc.gpsimd.tensor_scalar(nmr[:], mr[:], -1.0, 0.0, ALU.mult, ALU.add).then_inc(rstd_step, 1)
                if what == "add_bias":
                    pool.wait_ge(hn_done, b + 1)
                    seq = sequence(b)
                    nc.gpsimd.tensor_tensor(seq, seq, bo_rows[:].unsqueeze(1).to_broadcast([P, T, D]),
                                            ALU.add).then_inc(bias_added, 1)

            def step(b, par, half):
                walk(b, par, half, None, mask, None, split, spread)

            nc.gpsimd.memset(half_neg[:], -0.5).then_inc(half_set, 1)
            for i in range(2):
                nc.gpsimd.memset(v[i][:], 0.0).then_inc(v_set, 1)
            pool.wait_ge(v_set, 2)
            for i in range(2):
                nc.gpsimd.memset(v[i][:, :, :, HD:HD + 1], 1.0).then_inc(v_set, 1)
            pool.wait_ge(half_set, 1)
            pool.wait_ge(w_in, 8 * DMA)
            all_steps(pool, step)

        @block.vector
        def _(dve):
            def find_max(b, par, half, g, n):
                i, heads = max_unit(n)
                m = g * MAX_UNITS + n
                dve.wait_ge(max_out, b * NM + (m + 1))
                width = (i + 1) * P
                h0 = 4 * (g % 2) + heads[0]
                nc.vector.tensor_reduce(neg_max[par][:, g // 2, i, h0:h0 + len(heads)],
                                        max_ps[m % RING][:, 0:len(heads) * width].rearrange("p (h k) -> p h k", k=width),
                                        AX.X, ALU.max, negate=True).then_inc(max_read, 1)

            def statistics(b, par, half, what):
                if what != "statistics":
                    return
                if after(b, 0):
                    dve.wait_ge(rstd_step, b * RS)
                for t in range(T):
                    ins = nc.vector.bn_stats(bn[:, t, :], xt(b, t))
                ins.then_inc(bn_done, 1)
                dve.wait_ge(bn_done, b + 1)
                dve.sem_inc(dve_passed, 1)
                for t in range(T):
                    ins = nc.vector.bn_aggr(mean_var[:, t, :], bn[:, t, :])
                ins.then_inc(stats_done, 1)

            def side(b, par, half, what):
                if what == "project_v":
                    dve.wait_ge(turned, use(b, what))
                    if after(b, 0):
                        dve.wait_ge(pv_out, b * GROUPS)
                    nc.vector.tensor_tensor(v[1 - par][:, :, :, 0:HD],
                                            side_ps[:].rearrange("p (t h c) -> p t h c", t=T, c=HD),
                                            bv_rows[:].rearrange("p (h c) -> p h c", c=HD).unsqueeze(1).to_broadcast(
                                                [P, T, H, HD]), ALU.add).then_inc(side_read, 1)
                elif what == "output":
                    dve.wait_ge(turned, use(b, what))
                    dve.wait_ge(bias_added, b)
                    seq = sequence(b - 1)
                    nc.vector.tensor_tensor(seq, side_ps[:].rearrange("p (t d) -> p t d", d=D), seq,
                                            ALU.add).then_inc(side_read, 1)
                elif what[:-1] == "turn_o":
                    g = int(what[-1])
                    c = b - 1 if g >= 2 else b
                    dve.wait_ge(turned, use(b, what))
                    heads = side_ps[:].rearrange("p (t h c) -> p t h c", t=T, c=VW)
                    nc.vector.reciprocal(rden[:].unsqueeze(3), heads[:, :, :, HD:HD + 1]).then_inc(rden_done, 1)
                    dve.wait_ge(rden_done, c * GROUPS + (g + 1))
                    nc.vector.tensor_tensor(o[:, :, 4 * g * HD:4 * (g + 1) * HD].rearrange("p t (h c) -> p t h c", c=HD),
                                            heads[:, :, :, 0:HD], rden[:].unsqueeze(3).to_broadcast([P, T, 4, HD]),
                                            ALU.mult).then_inc(side_read, 1)

            def step(b, par, half):
                walk(b, par, half, find_max, None, None, side, statistics)

            for i in range(2):
                for ab in range(2):
                    nc.vector.memset(k_st[i][ab][:].rearrange("p r s -> p (r s)").bitcast(mybir.dt.uint32),
                                     0).then_inc(zeroed, 1)
            dve.wait_ge(v_set, 4)
            dve.wait_ge(w_in, 8 * DMA)
            all_steps(dve, step)


def macaron(nc, x_in, Wq, bq, Wk, bk, Wv, bv, Wo, bo, Wr, We, out):
    with ExitStack() as ctx:
        x = ctx.enter_context(nc.sbuf_tensor("x", [P, NSEQ * T * D], F32))
        consts = Consts(nc, ctx)
        placed = ctx.enter_context(nc.semaphore("consts_placed"))
        with nc.Block() as block:
            @block.sync
            def _(sp):
                for dst, src in consts.loads:
                    sp.dma_start(dst[:], src).then_inc(placed, DMA)
                sp.wait_ge(placed, len(consts.loads) * DMA)
        moe_layer(nc, "moe1", x, consts, Wr, We, x_in=x_in)
        attention(nc, x, consts, Wq, bq, Wk, bk, Wv, bv, Wo, bo)
        moe_layer(nc, "moe2", x, consts, Wr, We, out=out)


_INS = ["L0_attn_x", "L0_attn_Wq", "L0_attn_bq", "L0_attn_Wk", "L0_attn_bk", "L0_attn_Wv", "L0_attn_bv",
        "L0_attn_Wo", "L0_attn_bo", "L0_ffn_Wr", "L0_ffn_We"]


def kernel(**inputs):
    import concourse.bacc as bacc
    from concourse.bass_utils import run_bass_kernel_spmd

    arrays = {f"in_{n}": np.ascontiguousarray(inputs[n]) for n in _INS}
    nc = bacc.Bacc("TRN2", target_bir_lowering=False, num_devices=1)
    args = [nc.dram_tensor(n, list(a.shape), mybir.dt.from_np(a.dtype), kind="ExternalInput").ap()
            for n, a in arrays.items()]
    args.append(nc.dram_tensor("out", [NSEQ, S, D], F32, kind="ExternalOutput").ap())
    macaron(nc, *args)
    r = run_bass_kernel_spmd(nc, [arrays], core_ids=[0])
    return r.results[0]["out"]
```

```python
from contextlib import ExitStack

import numpy as np

import concourse.bass as bass
from concourse import mybir

F32 = mybir.dt.float32
U32 = mybir.dt.uint32
BF16 = mybir.dt.bfloat16
ALU = mybir.AluOpType
ACT = mybir.ActivationFunctionType
AX = mybir.AxisListType

P = 128
NSEQ, S, D = 16, 512, 128
T = S // P
H, HD = 16, 8
E, TOP_K = 8, 2
CAP = int(S * TOP_K / E * 1.5) + 1
EPS = 1e-5
DMA = 16

Q_PARTS = [0, 0, 0, 1, 1, 2]
K_PARTS = [0, 1, 2, 0, 1, 0]
HEAD_ROWS = len(Q_PARTS) * HD
ALIBI_ROW = 2 * HEAD_ROWS
STEP_ROW = ALIBI_ROW + 3
STEP = 32
STEPS = S // STEP - 1
SHIFT_ROW = STEP_ROW + STEPS
MAX_K = SHIFT_ROW
ALL_K = SHIFT_ROW + 2
PAIRS = H // 2
GROUPS = H // 4
VW = 32


def bf16_parts(a, n):
    parts, rest = [], np.asarray(a, np.float64)
    for _ in range(n):
        bits = rest.astype(np.float32).view(np.uint32)
        bits = (bits + 0x7FFF + ((bits >> 16) & 1)) & np.uint32(0xFFFF0000)
        parts.append((bits >> 16).astype(np.uint16))
        rest = rest - bits.view(np.float32).astype(np.float64)
    return parts


def after(b, n):
    return not isinstance(b, int) or b > n


class Consts:

    def __init__(self, nc, ctx):
        i = np.arange(P)
        one = bf16_parts(np.ones(1), 1)[0][0]
        eye = np.eye(P, dtype=np.float32)
        number = np.broadcast_to(np.arange(E).astype(np.float32), (P, E))
        before = (i[:, None] < i[None, :]).astype(np.float64)
        future = np.where(i[None, :] > i[:, None], -1e30, 0.0)
        b16 = np.concatenate([bf16_parts(a, 1)[0] for a in (eye, future, before, np.ones((P, P)))], axis=1)
        f32 = np.ascontiguousarray(np.concatenate([eye, number, np.full((P, T), -0.5, np.float32)], axis=1))
        self.loads = []
        self.placed = ctx.enter_context(nc.semaphore("consts_placed"))
        self.N_PLACED = 2 * DMA

        def place(name, data, dtype):
            src = nc.inline_tensor(np.ascontiguousarray(data), name + "_const")
            dst = ctx.enter_context(nc.sbuf_tensor(name, list(data.shape), dtype))
            src = src.ap() if dtype == F32 else src.ap().bitcast(dtype)
            self.loads.append((dst, src))
            return dst

        f = place("f32_consts", f32, F32)
        b = place("bf16_consts", b16, BF16)
        self.ident = f[:, 0:P]
        self.number = f[:, P:P + E]
        self.half_neg = f[:, P + E:P + E + T]
        self.ident_b = b[:, 0:P]
        self.future_b = b[:, P:2 * P]
        self.before_b = b[:, 2 * P:3 * P]
        self.ones_b = b[:, 3 * P:4 * P]

        slopes = (np.float32(2.0 ** (-8.0 / H)) ** np.arange(1, H + 1, dtype=np.float32)).astype(np.float64)
        block = np.arange(S)[None, :] // STEP
        self.k_rows = []
        for ab in range(2):
            rows = np.zeros((ALL_K - ALIBI_ROW, PAIRS, S), np.uint16)
            rows[0:3] = bf16_parts(slopes[ab::2, None] * np.arange(S)[None, :], 3)
            rows[3:3 + STEPS] = bf16_parts(np.where(block == np.arange(1, STEPS + 1)[:, None], -1e30, 0.0), 1)[0][:, None]
            rows[3 + STEPS + ab] = one
            self.k_rows.append(nc.inline_tensor(rows, f"k_rows_{ab}").ap().bitcast(BF16))
        rows = np.full((3 + STEPS, PAIRS, S), one, np.uint16)
        rows[3:] = np.where(block < np.arange(1, STEPS + 1)[:, None], one, 0)[:, None]
        self.q_rows = nc.inline_tensor(rows, "q_rows").ap().bitcast(BF16)
        self.zero_rows = nc.inline_tensor(np.zeros((HEAD_ROWS, PAIRS, S), np.uint16), "zero_rows").ap().bitcast(BF16)


def moe_layer(nc, tag, x, consts, Wr, We, x_in=None, out=None, ahead=None):
    with ExitStack() as ctx:
        def sb(name, shape, dt=F32):
            return ctx.enter_context(nc.sbuf_tensor(f"{tag}_{name}", shape, dt))

        def ps(name, shape):
            return ctx.enter_context(nc.psum_tensor(f"{tag}_{name}", shape, F32))

        def sem(name):
            return ctx.enter_context(nc.semaphore(f"{tag}_{name}"))

        we = sb("we", [P, E, D])
        wrT = sb("wrT", [P, E])
        bn = sb("bn", [P, T, 6])
        mean_var = sb("mean_var", [P, T, 2])
        veps = sb("veps", [P, T])
        rstd = sb("rstd", [P, T])
        nmr = sb("nmr", [P, T])
        hn = sb("hn", [P, T, D])
        hT = [sb(f"hT{i}", [P, S]) for i in range(2)]
        L = sb("L", [P, T, E])
        top = sb("top", [P, T, E])
        top_at = sb("top_at", [P, T, E], U32)
        first = sb("first", [P, T, E])
        second = sb("second", [P, T, E])
        picks = sb("picks", [P, T, E], BF16)
        gap = sb("gap", [P, T])
        egap = sb("egap", [P, T])
        den = sb("den", [P, T])
        w1 = sb("w1", [P, T])
        g2 = sb("g2", [P, T, E])
        g12 = sb("g12", [P, T, E])
        gw = sb("gw", [P, T, E])
        gates = [sb(f"gates{i}", [P, T, E]) for i in range(2)]
        HE = E // 2
        scaled = [sb(f"scaled{i}", [P, HE, D]) for i in range(2)]
        part2 = [sb(f"part2{i}", [P, 2, D]) for i in range(2)]
        part1 = [sb(f"part1{i}", [P, D]) for i in range(2)]

        lo_ps = [ps(f"lo{t}", [P, HE, D]) for t in range(T)]
        hi_ps = [ps(f"hi{t}", [P, HE, D]) for t in range(2)]
        hT_ps = ps("hT_ps", [P, S])
        route_ps = ps("route_ps", [P, 2, T, E])

        w_in = sem("w_in")
        x_loaded = [sem("x_loaded0"), sem("x_loaded1")]
        bn_done = sem("bn_done")
        stats_done = sem("stats_done")
        dve_passed = sem("dve_passed")
        eps_added = sem("eps_added")
        rstd_done = sem("rstd_done")
        nmr_done = sem("nmr_done")
        hn_done = sem("hn_done")
        hT_out = sem("hT_out")
        hT_copied = sem("hT_copied")
        logits_out = sem("logits_out")
        places_out = sem("places_out")
        route_step = sem("route_step")
        RT, GAP, PICKED = 12, 4, 7
        egap_done = sem("egap_done")
        lo_out, hi_out = sem("lo_out"), sem("hi_out")
        acc_step = sem("acc_step")
        scaled_done = sem("scaled_done")
        part_step = sem("part_step")
        stored = sem("stored")

        block = ctx.enter_context(nc.Block())

        def xt(b, t):
            return x[:, bass.ds((b * T + t) * D, D)]

        def sequence(b):
            return x[:, bass.ds(b * (T * D), T * D)].rearrange("p (t d) -> p t d", d=D)

        def added(b, t, e):
            n = b * T + t
            if isinstance(n, int) and n == 0 and e < 2:
                return e + 1
            if isinstance(n, int) and n == NSEQ * T - 1 and e >= 2:
                return n * HE + e + 1
            return n * HE + (-1, 1, 4, 6)[e]

        def halves_summed(b, t):
            n = b * T + t
            return 1 if isinstance(n, int) and n == 0 else n * 3

        def all_steps(eng, step):
            step(-1, 1, 0, False, True, True)
            step(0, 0, 1, True, True, True)
            with eng.Fori(0, NSEQ // 2 - 2) as i:
                step(2 * i + 1, 1, i + 1, True, True, True)
                step(2 * i + 2, 0, i + 2, True, True, True)
            step(NSEQ - 3, 1, NSEQ // 2 - 1, True, True, True)
            step(NSEQ - 2, 0, NSEQ // 2, True, True, False)
            step(NSEQ - 1, 1, NSEQ // 2, True, False, False)

        @block.sync
        def _(sp):
            if x_in is not None:
                src = x_in.rearrange("b (t p) d -> p (b t) d", p=P)

                def load(b, u):
                    sp.dma_start(sequence(b), src[:, bass.ds(b * T, T), :]).then_inc(x_loaded[u], DMA)

                load(0, 0)
                for dst, c in consts.loads:
                    sp.dma_start(dst[:], c).then_inc(consts.placed, DMA)
                load(1, 1)
            sp.dma_start(we[:], We.rearrange("e d f -> d e f")).then_inc(w_in, DMA)
            with nc.allow_non_contiguous_dma(reason="the router's 1024 weights, once"):
                sp.dma_start(wrT[:], Wr.rearrange("e d -> d e")).then_inc(w_in, DMA)
            if x_in is not None:
                with sp.Fori(1, NSEQ // 2) as i:
                    for u in range(2):
                        sp.wait_ge(x_loaded[u], i * DMA)
                        load(2 * i + u, u)
            if ahead:
                ahead.load(sp)
            if out is not None:
                dst = out.rearrange("b (t p) d -> p (b t) d", p=P)
                with sp.Fori(0, NSEQ - 1) as b:
                    sp.wait_ge(part_step, b * (3 * T) + (3 * T + 1))
                    sp.dma_start(dst[:, bass.ds(b * T, T), :], sequence(b)).then_inc(stored, DMA)
                sp.wait_ge(part_step, NSEQ * 3 * T)
                sp.dma_start(dst[:, (NSEQ - 1) * T:NSEQ * T, :], sequence(NSEQ - 1)).then_inc(stored, DMA)
                sp.wait_ge(stored, NSEQ * DMA)

        @block.tensor
        def _(pe):
            def turn_h(b, par):
                pe.wait_ge(hn_done, b + 1)
                if after(b, 0):
                    pe.wait_ge(hT_copied, b)
                for t in range(T):
                    mm = nc.tensor.transpose(hT_ps[:, t * P:(t + 1) * P], hn[:, t, :], consts.ident)
                mm.then_inc(hT_out, 1)

            def logits(b, par):
                pe.wait_ge(hT_copied, b + 1)
                if after(b, 0):
                    pe.wait_ge(route_step, b * RT)
                for t in range(T):
                    mm = nc.tensor.matmul(route_ps[:, 0, t, :], hT[par][:, t * P:(t + 1) * P], wrT[:],
                                          start=True, stop=True)
                mm.then_inc(logits_out, 1)

            def places(b):
                pe.wait_ge(route_step, b * RT + PICKED)
                nc.tensor.matmul(route_ps[:, 1, :, :], consts.before_b, picks[:], start=True, stop=False)
                for s in range(1, T):
                    mm = nc.tensor.matmul(route_ps[:, 1, s:T, :], consts.ones_b, picks[:, 0:T - s, :],
                                          start=False, stop=(s == T - 1))
                mm.then_inc(places_out, 1)

            def experts_lo(b, par, t):
                if after(b, 0):
                    pe.wait_ge(acc_step, added(b - 1, t, HE - 1))
                nc.tensor.matmul(lo_ps[t][:], hT[par][:, t * P:(t + 1) * P], we[:, 0:HE, :],
                                 start=True, stop=True).then_inc(lo_out, 1)

            def experts_hi(b, par, t):
                if after(b, 0) or t >= 2:
                    pe.wait_ge(scaled_done, b * T + t - 1)
                nc.tensor.matmul(hi_ps[t % 2][:], hT[par][:, t * P:(t + 1) * P], we[:, HE:E, :],
                                 start=True, stop=True).then_inc(hi_out, 1)

            def step(b, par, half, this, next1, next2):
                if next1:
                    turn_h(b + 1, 1 - par)
                if this:
                    experts_lo(b, par, 0)
                    experts_hi(b, par, 0)
                if next1:
                    logits(b + 1, 1 - par)
                if this:
                    for t in (1, 2):
                        experts_lo(b, par, t)
                        experts_hi(b, par, t)
                    experts_lo(b, par, 3)
                if next1:
                    places(b + 1)
                if this:
                    experts_hi(b, par, 3)

            pe.wait_ge(consts.placed, consts.N_PLACED)
            pe.wait_ge(w_in, 2 * DMA)
            all_steps(pe, step)

        @block.scalar
        def _(act):
            def normalise(b, par):
                act.wait_ge(nmr_done, b + 1)
                if after(b, 0):
                    act.wait_ge(hT_out, b)
                for t in range(T):
                    ins = nc.scalar.activation(hn[:, t, :], xt(b, t), ACT.Identity,
                                               bias=nmr[:, t:t + 1], scale=rstd[:, t:t + 1])
                ins.then_inc(hn_done, 1)

            def copy_hT(b, par):
                act.wait_ge(hT_out, b + 1)
                if after(b, 1):
                    act.wait_ge(hi_out, (b - 1) * T)
                nc.scalar.activation(hT[par][:], hT_ps[:], ACT.Copy).then_inc(hT_copied, 1)

            def exp_gap(b):
                act.wait_ge(route_step, b * RT + GAP)
                nc.scalar.activation(egap[:], gap[:], ACT.Exp).then_inc(egap_done, 1)

            def scale_products(b, par, t):
                act.wait_ge(hi_out, b * T + t + 1)
                if after(b, 0) or t >= 2:
                    act.wait_ge(part_step, halves_summed(b, t - 2) if t >= 2 else halves_summed(b - 1, t + T - 2))
                if t == 0:
                    act.wait_ge(route_step, b * RT + RT)
                for e in range(HE):
                    ins = nc.scalar.activation(scaled[t % 2][:, e, :], hi_ps[t % 2][:, e, :], ACT.Copy,
                                               scale=gates[par][:, t, HE + e:HE + e + 1])
                ins.then_inc(scaled_done, 1)

            def step(b, par, half, this, next1, next2):
                if next1:
                    copy_hT(b + 1, 1 - par)
                if after(b, 0):
                    scale_products(b - 1, 1 - par, 3)
                if this:
                    scale_products(b, par, 0)
                    scale_products(b, par, 1)
                if next2:
                    normalise(b + 2, par)
                if next1:
                    exp_gap(b + 1)
                if this:
                    scale_products(b, par, 2)

            normalise(0, 0)
            all_steps(act, step)
            scale_products(NSEQ - 1, 1, 3)

        @block.gpsimd
        def _(pool):
            def take_root(b):
                pool.wait_ge(eps_added, b + 1)
                if after(b, 0):
                    pool.wait_ge(hn_done, b)
                nc.gpsimd.tensor_tensor(rstd[:], veps[:], consts.half_neg, ALU.pow).then_inc(rstd_done, 1)

            def sum_parts(b, t):
                n = b * T + t
                pool.wait_ge(scaled_done, n + 1)
                nc.gpsimd.tensor_tensor(part2[t % 2][:], scaled[t % 2][:, 0:2, :], scaled[t % 2][:, 2:4, :],
                                        ALU.add).then_inc(part_step, 1)
                if t > 0:
                    add_parts(b, t - 1)
                elif after(b, 0):
                    add_parts(b - 1, T - 1)
                pool.wait_ge(part_step, halves_summed(b, t))
                nc.gpsimd.tensor_tensor(part1[t % 2][:], part2[t % 2][:, 0, :], part2[t % 2][:, 1, :],
                                        ALU.add).then_inc(part_step, 1)

            def add_parts(b, t):
                pool.wait_ge(part_step, (b * T + t) * 3 + 2)
                pool.wait_ge(acc_step, added(b, t, HE - 1))
                nc.gpsimd.tensor_tensor(xt(b, t), xt(b, t), part1[t % 2][:], ALU.add).then_inc(part_step, 1)

            def step(b, par, half, this, next1, next2):
                if next2:
                    take_root(b + 2)
                if this:
                    for t in range(T):
                        sum_parts(b, t)

            pool.wait_ge(consts.placed, consts.N_PLACED)
            take_root(0)
            if ahead:
                ahead.set_v(pool)
            all_steps(pool, step)
            add_parts(NSEQ - 1, T - 1)

        @block.vector
        def _(dve):
            def statistics(b, par, half):
                if x_in is not None:
                    dve.wait_ge(x_loaded[par], half * DMA + DMA)
                if after(b, 0):
                    dve.wait_ge(nmr_done, b)
                for t in range(T):
                    ins = nc.vector.bn_stats(bn[:, t, :], xt(b, t))
                ins.then_inc(bn_done, 1)

            def aggregate(b):
                dve.wait_ge(bn_done, b + 1)
                dve.sem_inc(dve_passed, 1)
                for t in range(T):
                    ins = nc.vector.bn_aggr(mean_var[:, t, :], bn[:, t, :])
                ins.then_inc(stats_done, 1)

            def add_eps(b):
                dve.wait_ge(stats_done, b + 1)
                if after(b, 0):
                    dve.wait_ge(rstd_done, b)
                nc.vector.tensor_scalar(veps[:], mean_var[:, :, 1], EPS, 0.0, ALU.add, ALU.add).then_inc(eps_added, 1)

            def shift_mean(b):
                dve.wait_ge(rstd_done, b + 1)
                nc.vector.scalar_tensor_tensor(out=nmr[:], in0=mean_var[:, :, 0], scalar=-1.0, in1=rstd[:],
                                               op0=ALU.mult, op1=ALU.mult).then_inc(nmr_done, 1)

            def over_e(a):
                return a.to_broadcast([P, T, E])

            number = consts.number.unsqueeze(1).to_broadcast([P, T, E])

            def route(b, par, n):
                done = b * RT
                if n == 0:
                    dve.wait_ge(logits_out, b + 1)
                    nc.vector.tensor_copy(L[:], route_ps[:, 0]).then_inc(route_step, 1)
                elif n == 1:
                    dve.wait_ge(route_step, done + 1)
                    dve.sem_inc(dve_passed, 1)
                    for t in range(T):
                        ins = nc.vector.max(top[:, t, :], L[:, t, :])
                    ins.then_inc(route_step, 1)
                elif n == 2:
                    dve.wait_ge(route_step, done + 2)
                    dve.sem_inc(dve_passed, 1)
                    for t in range(T):
                        ins = nc.vector.max_index(top_at[:, t, :], top[:, t, :], L[:, t, :])
                    ins.then_inc(route_step, 1)
                    nc.vector.tensor_tensor(gap[:], top[:, :, 1], top[:, :, 0], ALU.subtract).then_inc(
                        route_step, 1)
                elif n == 3:
                    dve.wait_ge(route_step, done + 3)
                    nc.vector.tensor_tensor(first[:], number, over_e(top_at[:, :, 0:1]), ALU.is_equal).then_inc(
                        route_step, 1)
                    nc.vector.tensor_tensor(second[:], number, over_e(top_at[:, :, 1:2]), ALU.is_equal).then_inc(
                        route_step, 1)
                elif n == 4:
                    dve.wait_ge(route_step, done + 6)
                    nc.vector.tensor_tensor(picks[:], first[:], second[:], ALU.add).then_inc(route_step, 1)
                elif n == 5:
                    dve.wait_ge(egap_done, b + 1)
                    nc.vector.tensor_scalar(den[:], egap[:], 1.0, 2.0, ALU.add, ALU.mult).then_inc(route_step, 1)
                    nc.vector.tensor_tensor(g2[:], second[:], over_e(egap[:].unsqueeze(2)), ALU.mult).then_inc(
                        route_step, 1)
                elif n == 6:
                    dve.wait_ge(route_step, done + 9)
                    nc.vector.reciprocal(w1[:], den[:])
                    nc.vector.tensor_tensor(g12[:], g2[:], first[:], ALU.add).then_inc(route_step, 1)
                elif n == 7:
                    dve.wait_ge(route_step, done + 10)
                    nc.vector.tensor_tensor(gw[:], g12[:], over_e(w1[:].unsqueeze(2)), ALU.mult).then_inc(
                        route_step, 1)
                elif n == 8:
                    dve.wait_ge(route_step, done + 11)
                    dve.wait_ge(places_out, b + 1)
                    if after(b, 1):
                        dve.wait_ge(scaled_done, (b - 1) * T)
                    nc.vector.scalar_tensor_tensor(out=gates[par][:], in0=route_ps[:, 1], scalar=float(CAP),
                                                   in1=gw[:], op0=ALU.is_lt, op1=ALU.mult).then_inc(
                        route_step, 1)

            def add_expert(b, par, t, e):
                if e > 0:
                    dve.wait_ge(acc_step, added(b, t, e - 1))
                nc.vector.scalar_tensor_tensor(out=xt(b, t), in0=lo_ps[t][:, e, :],
                                               scalar=gates[par][:, t, e:e + 1], in1=xt(b, t),
                                               op0=ALU.mult, op1=ALU.add).then_inc(acc_step, 1)

            ROUTE_AFTER = {(1, 0): [0], (1, 1): [1], (1, 2): [2], (1, 3): [3], (2, 0): [4], (2, 2): [5],
                           (2, 3): [6], (3, 0): [7], (3, 3): [8]}

            def step(b, par, half, this, next1, next2):
                if next2:
                    statistics(b + 2, par, half)
                for t in range(T):
                    if this:
                        dve.wait_ge(lo_out, b * T + t + 1)
                        if t == 0:
                            dve.wait_ge(route_step, b * RT + RT)
                            dve.wait_ge(hn_done, b + 1)
                    for k in range(HE):
                        if this and k % 2 == 0:
                            add_expert(b, par, t, k // 2)
                        elif this and t > 0:
                            add_expert(b, par, t - 1, 2 + k // 2)
                        elif this and after(b, 0):
                            add_expert(b - 1, 1 - par, T - 1, 2 + k // 2)
                        if next1:
                            for n in ROUTE_AFTER.get((t, k), []):
                                route(b + 1, 1 - par, n)
                        if next2 and (t, k) == (0, 0):
                            aggregate(b + 2)
                        if next2 and (t, k) == (0, 1):
                            add_eps(b + 2)
                        if next2 and (t, k) == (1, 0):
                            shift_mean(b + 2)

            dve.wait_ge(consts.placed, consts.N_PLACED)
            statistics(0, 0, 0)
            aggregate(0)
            add_eps(0)
            shift_mean(0)
            all_steps(dve, step)
            for e in (2, 3):
                add_expert(NSEQ - 1, 1, T - 1, e)


SIDE_WORK = [
    {2: "shift_hi", 5: "turn_o2"},
    {1: "turn_h", 4: "project_q", 6: "turn_o3", 8: "project_k"},
    {0: "turn_o", 3: "shift_lo", 5: "turn_o0", 7: "project_v"},
    {0: "output", 5: "turn_o1"},
]
PREPARE = {(0, 1): "statistics", (0, 2): "aggregate", (0, 3): "add_eps", (0, 4): "take_root", (0, 6): "shift_mean",
           (0, 7): "normalise0", (0, 8): "normalise1", (0, 9): "normalise2", (0, 10): "normalise3", (1, 5): "split_q0", (1, 6): "split_q1", (1, 7): "split_q2", (1, 8): "split_q3",
           (1, 9): "split_k0", (1, 10): "split_k1", (2, 0): "split_k2", (2, 2): "split_k3", (3, 4): "add_bias"}
PV_AFTER = {3: 0, 5: 1, 7: 2, 9: 3}
MAX_UNITS = 11
EXP_UNITS = 10


def max_unit(n):
    return [(0, [0, 1, 2, 3]), (1, [0, 1]), (1, [2, 3]),
            (2, [0]), (2, [1]), (2, [2]), (2, [3]), (3, [0]), (3, [1]), (3, [2]), (3, [3])][n]


def exp_unit(n):
    pair, u = divmod(n, 5)
    return pair, [[(0, 0, 0)], [(0, 1, 0), (0, 3, 3 * P)], [(0, 2, 0), (1, 2, 2 * P)],
                  [(1, 0, 0)], [(1, 1, 0), (1, 3, 3 * P)]][u]


class AttentionOperands:

    def __init__(self, nc, ctx, consts, Wq, bq, Wk, bk, Wv, bv, Wo, bo):
        def sb(name, shape, dt=F32):
            return ctx.enter_context(nc.sbuf_tensor(f"att_{name}", shape, dt))

        self.nc, self.consts = nc, consts
        self.w = {n: sb(n, [P, D]) for n in ("wq", "wk", "wv", "wo")}
        self.weights = list(zip(self.w.values(), (Wq, Wk, Wv, Wo)))
        self.bq_col, self.bk_col = sb("bq_col", [P, 1]), sb("bk_col", [P, 1])
        self.bv_rows, self.bo_rows = sb("bv_rows", [P, D]), sb("bo_rows", [P, D])
        self.biases = (bq, bk, bv, bo)
        self.q_st = [sb(f"q_st{i}", [P, PAIRS, S], BF16) for i in range(2)]
        self.k_st = [[sb(f"k_st{i}{ab}", [P, PAIRS, S], BF16) for ab in range(2)] for i in range(2)]
        self.v = [sb(f"v{i}", [P, T, H, VW]) for i in range(2)]
        self.weights_in = ctx.enter_context(nc.semaphore("att_weights_in"))
        self.rows_in = ctx.enter_context(nc.semaphore("att_rows_in"))
        self.v_set = ctx.enter_context(nc.semaphore("att_v_set"))
        self.N_WEIGHTS, self.N_ROWS, self.N_V = 8 * DMA, 10 * DMA, 4

    def load(self, eng):
        for dst, src in self.weights:
            eng.dma_start(dst[:], src).then_inc(self.weights_in, DMA)
        bq, bk, bv, bo = self.biases
        eng.dma_start(self.bq_col[:], bq.rearrange("(p a) -> p a", a=1)).then_inc(self.weights_in, DMA)
        eng.dma_start(self.bk_col[:], bk.rearrange("(p a) -> p a", a=1)).then_inc(self.weights_in, DMA)
        eng.dma_start(self.bv_rows[:], bv.partition_broadcast(P)).then_inc(self.weights_in, DMA)
        eng.dma_start(self.bo_rows[:], bo.partition_broadcast(P)).then_inc(self.weights_in, DMA)
        for i in range(2):
            eng.dma_start(self.q_st[i][ALIBI_ROW:SHIFT_ROW], self.consts.q_rows).then_inc(self.rows_in, DMA)
            for ab in range(2):
                k_st = self.k_st[i][ab]
                eng.dma_start(k_st[ALIBI_ROW:ALL_K], self.consts.k_rows[ab]).then_inc(self.rows_in, DMA)
                eng.dma_start(k_st[(1 - ab) * HEAD_ROWS:(2 - ab) * HEAD_ROWS],
                              self.consts.zero_rows).then_inc(self.rows_in, DMA)

    def set_v(self, pool):
        for i in range(2):
            self.nc.gpsimd.memset(self.v[i][:], 0.0).then_inc(self.v_set, 1)
        pool.wait_ge(self.v_set, 2)
        for i in range(2):
            self.nc.gpsimd.memset(self.v[i][:, :, :, HD:HD + 1], 1.0).then_inc(self.v_set, 1)


def attention(nc, x, consts, ops):
    scratch = nc.dram_tensor("qk_parts", [2, 2, PAIRS, 2, len(Q_PARTS), HD, S], BF16, kind="Internal").ap()
    w, q_st, k_st, v = ops.w, ops.q_st, ops.k_st, ops.v
    bq_col, bk_col, bv_rows, bo_rows = ops.bq_col, ops.bk_col, ops.bv_rows, ops.bo_rows
    with ExitStack() as ctx:
        def sb(name, shape, dt=F32):
            return ctx.enter_context(nc.sbuf_tensor(f"att_{name}", shape, dt))

        def ps(name, shape):
            return ctx.enter_context(nc.psum_tensor(f"att_{name}", shape, F32))

        def sem(name):
            return ctx.enter_context(nc.semaphore(f"att_{name}"))

        def both(f):
            return [f(0), f(1)]

        bq_scaled = sb("bq_scaled", [P, 1])
        bn = sb("bn", [P, T, 6])
        mean_var = sb("mean_var", [P, T, 2])
        veps, rstd, nmr = sb("veps", [P, T]), sb("rstd", [P, T]), sb("nmr", [P, T])
        hn = sb("hn", [P, T, D])
        hT = both(lambda i: sb(f"hT{i}", [P, S]))
        qk = both(lambda i: sb(f"qk{i}", [P, S]))
        rest = both(lambda i: sb(f"rest{i}", [P, S]))
        parts = both(lambda i: sb(f"parts{i}", [P, 3, S], BF16))
        neg_max = both(lambda i: sb(f"neg_max{i}", [P, 2, 2, PAIRS // 2, T], BF16))
        shift = sb("shift", [T * H // 2, P], BF16)
        probs = both(lambda i: sb(f"probs{i}", [P, EXP_UNITS, S]))
        oT = sb("oT", [P, S])
        rden = sb("rden", [P, T, 4])
        o = sb("o", [P, T, D])
        o_fm = sb("o_fm", [P, S])

        RING = 3
        max_ps = [ps(f"max{i}", [P, S]) for i in range(RING)]
        exp_ps = [ps(f"exp{i}", [P, S]) for i in range(RING)]
        pv_ps = ps("pv", [P, S])
        side_ps = ps("side", [P, S])

        bias_scaled = sem("bias_scaled")
        pool_passed, dve_passed = sem("pool_passed"), sem("dve_passed")
        bn_done, stats_done, eps_added = sem("bn_done"), sem("stats_done"), sem("eps_added")
        rstd_done = sem("rstd_done")
        nmr_done = sem("nmr_done")
        hn_done = sem("hn_done")
        bias_added = sem("bias_added")
        split_step = both(lambda s: sem(f"split_step{s}"))
        scratch_in = both(lambda i: both(lambda s: sem(f"scratch_in{i}{s}")))
        stack_in = both(lambda i: both(lambda hf: sem(f"stack_in{i}{hf}")))
        shift_in = both(lambda i: both(lambda hf: sem(f"shift_in{i}{hf}")))
        SCRATCH_DMAS = len(Q_PARTS)
        STACK_DMAS = 3
        SHIFT_DMAS = 2
        max_out = sem("max_out")
        max_read = sem("max_read")
        exp_out = sem("exp_out")
        exp_done = sem("exp_done")
        masked = sem("masked")
        pv_out = sem("pv_out")
        pv_read = sem("pv_read")
        turned = sem("turned")
        side_read = sem("side_read")
        rden_done = sem("rden_done")
        NM, NE = GROUPS * MAX_UNITS, GROUPS * EXP_UNITS

        order = [what for g in SIDE_WORK for what in g.values()]

        def present(b, what):
            if not isinstance(b, int):
                return True
            offset = {"turn_h": 2, "project_q": 2, "project_k": 2, "project_v": 1, "shift_lo": 1, "shift_hi": 0,
                      "turn_o2": -1, "turn_o3": -1, "turn_o": -1, "output": -1, "turn_o0": 0, "turn_o1": 0}[what]
            return 0 <= b + offset < NSEQ

        L = len(order)
        before = {-2: 0}
        for n in range(-1, 3):
            before[n] = before[n - 1] + sum(present(n - 1, what) for what in order)
        before[NSEQ - 2] = before[2] + (NSEQ - 4) * L
        for n in range(NSEQ - 1, NSEQ + 2):
            before[n] = before[n - 1] + sum(present(n - 1, what) for what in order)

        def use(b, what):
            here = order[:order.index(what) + 1]
            if isinstance(b, int) and b in before:
                return before[b] + sum(present(b, w) for w in here)
            return b * L + (before[2] - 2 * L + len(here))

        block = ctx.enter_context(nc.Block())

        def xt(b, t):
            return x[:, bass.ds((b * T + t) * D, D)]

        def sequence(b):
            return x[:, bass.ds(b * (T * D), T * D)].rearrange("p (t d) -> p t d", d=D)

        def all_steps(eng, step):
            for b in range(-2, 2):
                step(b, b % 2, b // 2)
            with eng.Fori(1, NSEQ // 2 - 1) as i:
                step(2 * i, 0, i)
                step(2 * i + 1, 1, i)
            for b in range(NSEQ - 2, NSEQ + 1):
                step(b, b % 2, b // 2)

        def there(b):
            return not isinstance(b, int) or 0 <= b < NSEQ

        def walk(b, par, half, on_max=None, on_exp=None, on_pv=None, on_side=None, on_prepare=None):
            for g in range(GROUPS):
                for n in range(MAX_UNITS):
                    if on_max and there(b + 1):
                        on_max(b + 1, 1 - par, half + par, g, n)
                    if on_exp and n < EXP_UNITS and there(b):
                        on_exp(b, par, half, g, n)
                    if on_prepare and (g, n) in PREPARE and there(b + 2):
                        on_prepare(b + 2, par, half + 1, PREPARE[g, n])
                    if on_side and n in SIDE_WORK[g] and present(b, SIDE_WORK[g][n]):
                        on_side(b, par, half, SIDE_WORK[g][n])
                    if on_pv and n in PV_AFTER:
                        if g > 0 and there(b):
                            on_pv(b, par, g - 1, PV_AFTER[n])
                        if g == 0 and there(b - 1):
                            on_pv(b - 1, 1 - par, GROUPS - 1, PV_AFTER[n])

        def dve_splits(b, which):
            return isinstance(b, int) and b == 0 and which == "k"

        def split(eng, ops_of, passed, b, par, half, what):
            s, n = int(what[-2] == "k"), int(what[-1])
            if n == 0:
                eng.wait_ge(side_read, use(b - 2, "project_k" if s else "project_q"))
                if after(b, 0):
                    eng.wait_ge(scratch_in[1 - par][s], (half + par) * (SCRATCH_DMAS * DMA))
                eng.sem_inc(passed, 1)
                ins = ops_of.tensor_scalar(parts[s][:, 0], qk[s][:], 1.0, 1.0, ALU.mult, ALU.mult)
            elif n == 1:
                eng.wait_ge(split_step[s], b * 4 + 1)
                ins = ops_of.tensor_tensor(rest[s][:], qk[s][:], parts[s][:, 0], ALU.subtract)
            elif n == 2:
                eng.wait_ge(split_step[s], b * 4 + 2)
                eng.sem_inc(passed, 1)
                ins = ops_of.tensor_scalar(parts[s][:, 1], rest[s][:], 1.0, 1.0, ALU.mult, ALU.mult)
            else:
                eng.wait_ge(split_step[s], b * 4 + 3)
                ins = ops_of.tensor_tensor(parts[s][:, 2], rest[s][:], parts[s][:, 1], ALU.subtract)
            ins.then_inc(split_step[s], 1)

        @block.sync
        def _(sp):
            def store_parts(b, par, half, side):
                which = (Q_PARTS, K_PARTS)[side]
                for term in sorted(range(len(which)), key=lambda t: which[t]):
                    part = which[term]
                    sp.wait_ge(split_step[side], b * 4 + (1, 3, 4)[part])
                    sp.dma_start(scratch[par, side, :, :, term].rearrange("r u d s -> (r u) d s"),
                                 parts[side][:, part]).then_inc(scratch_in[par][side], DMA)

            def stack(b, par, half, hf):
                if hf == 0:
                    for side in range(2):
                        sp.wait_ge(scratch_in[par][side], half * (SCRATCH_DMAS * DMA) + SCRATCH_DMAS * DMA)
                if after(b, 1):
                    sp.wait_ge(exp_out, (b - 2) * NE + (hf + 1) * NE // 2)
                pairs = slice(hf * PAIRS // 2, (hf + 1) * PAIRS // 2)
                sp.dma_start(q_st[par][0:2 * HEAD_ROWS, pairs, :],
                             scratch[par, 0, pairs].rearrange("r u t d s -> (u t d) r s")).then_inc(
                    stack_in[par][hf], DMA)
                for ab in range(2):
                    sp.dma_start(k_st[par][ab][ab * HEAD_ROWS:(ab + 1) * HEAD_ROWS, pairs, :],
                                 scratch[par, 1, pairs, ab].rearrange("r t d s -> (t d) r s")).then_inc(
                        stack_in[par][hf], DMA)

            def place_shift(b, par, half, hf):
                sp.wait_ge(side_read, use(b if hf else b - 1, "shift_hi" if hf else "shift_lo"))
                pairs = slice(hf * PAIRS // 2, (hf + 1) * PAIRS // 2)
                for ab in range(2):
                    rows = PAIRS // 2 * T
                    sp.dma_start(q_st[par][SHIFT_ROW + ab:SHIFT_ROW + ab + 1, pairs, :],
                                 shift[ab * rows:(ab + 1) * rows, :]).then_inc(shift_in[par][hf], DMA)

            def step(b, par, half):
                if there(b):
                    place_shift(b, par, half, 1)
                if there(b + 2):
                    store_parts(b + 2, par, half + 1, 0)
                    store_parts(b + 2, par, half + 1, 1)
                    stack(b + 2, par, half + 1, 0)
                if there(b + 1):
                    place_shift(b + 1, 1 - par, half, 0)
                if there(b + 2):
                    stack(b + 2, par, half + 1, 1)

            all_steps(sp, step)

        @block.tensor
        def _(pe):
            def take_max_scores(b, par, half, g, n):
                i, heads = max_unit(n)
                m = g * MAX_UNITS + n
                if n == 0 and g in (0, 2):
                    pe.wait_ge(stack_in[par][g // 2], half * (STACK_DMAS * DMA) + STACK_DMAS * DMA)
                if m >= RING:
                    pe.wait_ge(max_read, b * NM + (m - RING + 1))
                elif after(b, 0):
                    last = max(k for k in range(NM) if k % RING == m % RING)
                    pe.wait_ge(max_read, (b - 1) * NM + (last + 1))
                width = (i + 1) * P
                for c, hh in enumerate(heads):
                    r, ab = divmod(4 * g + hh, 2)
                    nc.tensor.matmul(max_ps[m % RING][:, c * width:(c + 1) * width],
                                     q_st[par][0:MAX_K, r, i * P:(i + 1) * P], k_st[par][ab][0:MAX_K, r, 0:width],
                                     start=True, stop=False)
                    mm = nc.tensor.matmul(max_ps[m % RING][:, (c + 1) * width - P:(c + 1) * width],
                                          consts.ident_b, consts.future_b, start=False, stop=True)
                mm.then_inc(max_out, 1)

            def take_exp_scores(b, par, half, g, n):
                pair, pieces = exp_unit(n)
                m = g * EXP_UNITS + n
                if n == 0 and g in (0, 2):
                    pe.wait_ge(shift_in[par][g // 2], half * (SHIFT_DMAS * DMA) + SHIFT_DMAS * DMA)
                if m >= RING:
                    pe.wait_ge(exp_done, b * NE + (m - RING + 1))
                elif after(b, 0):
                    last = max(k for k in range(NE) if k % RING == m % RING)
                    pe.wait_ge(exp_done, (b - 1) * NE + (last + 1))
                r = 2 * g + pair
                for ab, j, c in pieces:
                    mm = nc.tensor.matmul(exp_ps[m % RING][:, c:c + S - j * P],
                                          k_st[par][ab][0:ALL_K, r, j * P:(j + 1) * P],
                                          q_st[par][0:ALL_K, r, j * P:S], start=True, stop=True)
                mm.then_inc(exp_out, 1)

            def weigh_values(b, par, g, j):
                if j == 0:
                    pe.wait_ge(masked, b * NE + (g + 1) * EXP_UNITS)
                    if g > 0 or after(b, 0):
                        pe.wait_ge(pv_read, b * GROUPS + g)
                    if g == 0:
                        pe.wait_ge(side_read, use(b - 1, "project_v"))
                for hh in range(4):
                    pair, ab = divmod(hh, 2)
                    n, c = next((n, c) for n in range(EXP_UNITS) for a, jj, c in exp_unit(n)[1]
                                if exp_unit(n)[0] == pair and (a, jj) == (ab, j))
                    mm = nc.tensor.matmul(pv_ps[VW * hh:VW * (hh + 1), j * P:S], v[par][:, j, 4 * g + hh, :],
                                          probs[g % 2][:, n, c:c + S - j * P], start=(j == 0), stop=(j == T - 1))
                if j == T - 1:
                    mm.then_inc(pv_out, 1)

            def side(b, par, half, what):
                n = use(b, what)
                if not isinstance(n, int) or n > 1:
                    pe.wait_ge(side_read, n - 1)
                if what == "turn_h":
                    pe.wait_ge(hn_done, (b + 2) * T + T)
                    for t in range(T):
                        mm = nc.tensor.transpose(side_ps[:, t * P:(t + 1) * P], hn[:, t, :], consts.ident)
                elif what in ("project_q", "project_k"):
                    mm = nc.tensor.matmul(side_ps[:], w["wq" if what == "project_q" else "wk"][:], hT[par][:],
                                          start=True, stop=True)
                elif what == "project_v":
                    for t in range(T):
                        mm = nc.tensor.matmul(side_ps[:, t * P:(t + 1) * P], hT[1 - par][:, t * P:(t + 1) * P],
                                              w["wv"][:], start=True, stop=True)
                elif what in ("shift_lo", "shift_hi"):
                    hi = what == "shift_hi"
                    pe.wait_ge(max_read, (b if hi else b + 1) * NM + (NM if hi else NM // 2))
                    mm = nc.tensor.transpose(side_ps[0:T * H // 2, 0:P // 2].bitcast(BF16),
                                             neg_max[par if hi else 1 - par][:, int(hi)], consts.ident_b)
                elif what == "turn_o":
                    pe.wait_ge(side_read, use(b, "turn_o3"))
                    for t in range(T):
                        mm = nc.tensor.transpose(side_ps[:, t * P:(t + 1) * P], o[:, t, :], consts.ident)
                elif what == "output":
                    for t in range(T):
                        mm = nc.tensor.matmul(side_ps[:, t * P:(t + 1) * P], o_fm[:, t * P:(t + 1) * P],
                                              w["wo"][:], start=True, stop=True)
                else:
                    g = int(what[-1])
                    pe.wait_ge(pv_read, (b - 1 if g >= 2 else b) * GROUPS + (g + 1))
                    for t in range(T):
                        mm = nc.tensor.transpose(side_ps[:, t * P:(t + 1) * P], oT[:, t * P:(t + 1) * P], consts.ident)
                mm.then_inc(turned, 1)

            def step(b, par, half):
                walk(b, par, half, take_max_scores, take_exp_scores, weigh_values, side)

            pe.wait_ge(ops.weights_in, ops.N_WEIGHTS)
            pe.wait_ge(ops.rows_in, ops.N_ROWS)
            pe.wait_ge(ops.v_set, ops.N_V)
            all_steps(pe, step)

        @block.scalar
        def _(act):
            def exponentiate(b, par, half, g, n):
                m = g * EXP_UNITS + n
                act.wait_ge(exp_out, b * NE + (m + 1))
                if n == 0:
                    if g >= 2:
                        act.wait_ge(pv_out, b * GROUPS + (g - 1))
                    elif after(b, 0):
                        act.wait_ge(pv_out, (b - 1) * GROUPS + (g + 3))
                nc.scalar.activation(probs[g % 2][:, n, :], exp_ps[m % RING][:], ACT.Exp).then_inc(exp_done, 1)

            def copy_values(b, par, g, j):
                if j < T - 1:
                    return
                act.wait_ge(pv_out, b * GROUPS + (g + 1))
                if g > 0 or after(b, 0):
                    act.wait_ge(turned, use(b + 1 if g == 3 else b, f"turn_o{(g - 1) % GROUPS}"))
                nc.scalar.activation(oT[:], pv_ps[:], ACT.Copy).then_inc(pv_read, 1)

            def side(b, par, half, what):
                if what in ("project_v", "output") or what[:-1] == "turn_o":
                    return
                act.wait_ge(turned, use(b, what))
                if what == "turn_h":
                    nc.scalar.activation(hT[par][:], side_ps[:], ACT.Copy).then_inc(side_read, 1)
                elif what in ("project_q", "project_k"):
                    s = int(what == "project_k")
                    if after(b, -2):
                        act.wait_ge(split_step[s], (b + 1) * 4 + 4)
                    nc.scalar.activation(qk[s][:], side_ps[:], ACT.Identity,
                                         bias=(bk_col if s else bq_scaled)[:],
                                         scale=1.0 if s else HD ** -0.5).then_inc(side_read, 1)
                elif what in ("shift_lo", "shift_hi"):
                    hi = what == "shift_hi"
                    if hi:
                        act.wait_ge(shift_in[par][0], (half + 1) * (SHIFT_DMAS * DMA))
                    elif after(b, -1):
                        act.wait_ge(shift_in[par][1], (half + 1) * (SHIFT_DMAS * DMA))
                    nc.scalar.activation(shift[:], side_ps[0:T * H // 2, 0:P // 2].bitcast(BF16),
                                         ACT.Copy).then_inc(side_read, 1)
                elif what == "turn_o":
                    nc.scalar.activation(o_fm[:], side_ps[:], ACT.Copy).then_inc(side_read, 1)

            def normalise(b, par, half, what):
                if what[:-1] != "normalise":
                    return
                t = int(what[-1])
                if t == 0:
                    act.wait_ge(nmr_done, b + 1)
                    if after(b, 0):
                        act.wait_ge(turned, use(b - 3, "turn_h"))
                nc.scalar.activation(hn[:, t, :], xt(b, t), ACT.Identity,
                                     bias=nmr[:, t:t + 1], scale=rstd[:, t:t + 1]).then_inc(hn_done, 1)

            def step(b, par, half):
                walk(b, par, half, None, exponentiate, copy_values, side, normalise)

            act.wait_ge(ops.weights_in, ops.N_WEIGHTS)
            nc.scalar.activation(bq_scaled[:], bq_col[:], ACT.Copy, scale=HD ** -0.5).then_inc(bias_scaled, 1)
            act.wait_ge(bias_scaled, 1)
            all_steps(act, step)

        @block.gpsimd
        def _(pool):
            def mask(b, par, half, g, n):
                pieces = exp_unit(n)[1]
                view = probs[g % 2][:, n, :].rearrange("p (a c) -> p a c", c=P)
                blocks = [c // P for _, _, c in pieces]
                view = view[:, 0:1, :] if len(blocks) == 1 else view[:, 0:blocks[1] + 1:blocks[1], :]
                pool.wait_ge(exp_done, b * NE + (g * EXP_UNITS + n + 1))
                pool.sem_inc(pool_passed, 1)
                nc.gpsimd.affine_select(out=view, in_=view, compare_op=ALU.is_ge, fill=0.0, base=0,
                                        pattern=[[0, len(blocks)], [1, P]], channel_multiplier=-1).then_inc(masked, 1)

            def prepare(b, par, half, what):
                if what[:-2] == "split_":
                    if not dve_splits(b, what[-2]):
                        split(pool, nc.gpsimd, pool_passed, b, par, half, what)
                elif what == "take_root":
                    pool.wait_ge(eps_added, b + 1)
                    if after(b, 0):
                        pool.wait_ge(hn_done, b * T)
                    nc.gpsimd.tensor_tensor(rstd[:], veps[:], consts.half_neg, ALU.pow).then_inc(rstd_done, 1)
                elif what == "add_bias":
                    pool.wait_ge(hn_done, b * T + T)
                    seq = sequence(b)
                    nc.gpsimd.tensor_tensor(seq, seq, bo_rows[:].unsqueeze(1).to_broadcast([P, T, D]),
                                            ALU.add).then_inc(bias_added, 1)

            def step(b, par, half):
                walk(b, par, half, on_exp=mask, on_prepare=prepare)

            pool.wait_ge(ops.weights_in, ops.N_WEIGHTS)
            all_steps(pool, step)

        @block.vector
        def _(dve):
            def find_max(b, par, half, g, n):
                i, heads = max_unit(n)
                m = g * MAX_UNITS + n
                dve.wait_ge(max_out, b * NM + (m + 1))
                width = (i + 1) * P
                r0, ab = divmod(heads[0], 2)
                r0 += 2 * (g % 2)
                n_r, n_ab = (len(heads) + 1) // 2, min(len(heads), 2)
                nc.vector.tensor_reduce(neg_max[par][:, g // 2, ab:ab + n_ab, r0:r0 + n_r, i].rearrange("p a r -> p r a"),
                                        max_ps[m % RING][:, 0:len(heads) * width].rearrange(
                                            "p (r a k) -> p r a k", r=n_r, k=width),
                                        AX.X, ALU.max, negate=True).then_inc(max_read, 1)

            def statistics(b, par, half, what):
                if what[:-2] == "split_" and dve_splits(b, what[-2]):
                    split(dve, nc.vector, dve_passed, b, par, half, what)
                elif what == "statistics":
                    if after(b, 0):
                        dve.wait_ge(nmr_done, b)
                    for t in range(T):
                        ins = nc.vector.bn_stats(bn[:, t, :], xt(b, t))
                    ins.then_inc(bn_done, 1)
                elif what == "aggregate":
                    dve.wait_ge(bn_done, b + 1)
                    dve.sem_inc(dve_passed, 1)
                    for t in range(T):
                        ins = nc.vector.bn_aggr(mean_var[:, t, :], bn[:, t, :])
                    ins.then_inc(stats_done, 1)
                elif what == "add_eps":
                    dve.wait_ge(stats_done, b + 1)
                    if after(b, 0):
                        dve.wait_ge(rstd_done, b)
                    nc.vector.tensor_scalar(veps[:], mean_var[:, :, 1], EPS, 0.0, ALU.add, ALU.add).then_inc(eps_added, 1)
                elif what == "shift_mean":
                    dve.wait_ge(rstd_done, b + 1)
                    nc.vector.scalar_tensor_tensor(out=nmr[:], in0=mean_var[:, :, 0], scalar=-1.0, in1=rstd[:],
                                                   op0=ALU.mult, op1=ALU.mult).then_inc(nmr_done, 1)

            def side(b, par, half, what):
                if what == "project_v":
                    dve.wait_ge(turned, use(b, what))
                    if after(b, 0):
                        dve.wait_ge(pv_out, b * GROUPS)
                    nc.vector.tensor_tensor(v[1 - par][:, :, :, 0:HD],
                                            side_ps[:].rearrange("p (t h c) -> p t h c", t=T, c=HD),
                                            bv_rows[:].rearrange("p (h c) -> p h c", c=HD).unsqueeze(1).to_broadcast(
                                                [P, T, H, HD]), ALU.add).then_inc(side_read, 1)
                elif what == "output":
                    dve.wait_ge(turned, use(b, what))
                    dve.wait_ge(bias_added, b)
                    seq = sequence(b - 1)
                    nc.vector.tensor_tensor(seq, side_ps[:].rearrange("p (t d) -> p t d", d=D), seq,
                                            ALU.add).then_inc(side_read, 1)
                elif what[:-1] == "turn_o":
                    g = int(what[-1])
                    c = b - 1 if g >= 2 else b
                    dve.wait_ge(turned, use(b, what))
                    heads = side_ps[:].rearrange("p (t h c) -> p t h c", t=T, c=VW)
                    nc.vector.reciprocal(rden[:].unsqueeze(3), heads[:, :, :, HD:HD + 1]).then_inc(rden_done, 1)
                    dve.wait_ge(rden_done, c * GROUPS + (g + 1))
                    nc.vector.tensor_tensor(o[:, :, 4 * g * HD:4 * (g + 1) * HD].rearrange("p t (h c) -> p t h c", c=HD),
                                            heads[:, :, :, 0:HD], rden[:].unsqueeze(3).to_broadcast([P, T, 4, HD]),
                                            ALU.mult).then_inc(side_read, 1)

            def step(b, par, half):
                walk(b, par, half, find_max, None, None, side, statistics)

            dve.wait_ge(ops.weights_in, ops.N_WEIGHTS)
            dve.wait_ge(ops.v_set, ops.N_V)
            all_steps(dve, step)


def macaron(nc, x_in, Wq, bq, Wk, bk, Wv, bv, Wo, bo, Wr, We, out):
    with ExitStack() as ctx:
        x = ctx.enter_context(nc.sbuf_tensor("x", [P, NSEQ * T * D], F32))
        consts = Consts(nc, ctx)
        ops = AttentionOperands(nc, ctx, consts, Wq, bq, Wk, bk, Wv, bv, Wo, bo)
        moe_layer(nc, "moe1", x, consts, Wr, We, x_in=x_in, ahead=ops)
        attention(nc, x, consts, ops)
        moe_layer(nc, "moe2", x, consts, Wr, We, out=out)


_INS = ["L0_attn_x", "L0_attn_Wq", "L0_attn_bq", "L0_attn_Wk", "L0_attn_bk", "L0_attn_Wv", "L0_attn_bv",
        "L0_attn_Wo", "L0_attn_bo", "L0_ffn_Wr", "L0_ffn_We"]


def kernel(**inputs):
    import concourse.bacc as bacc
    from concourse.bass_utils import run_bass_kernel_spmd

    arrays = {f"in_{n}": np.ascontiguousarray(inputs[n]) for n in _INS}
    nc = bacc.Bacc("TRN2", target_bir_lowering=False, num_devices=1)
    args = [nc.dram_tensor(n, list(a.shape), mybir.dt.from_np(a.dtype), kind="ExternalInput").ap()
            for n, a in arrays.items()]
    args.append(nc.dram_tensor("out", [NSEQ, S, D], F32, kind="ExternalOutput").ap())
    macaron(nc, *args)
    r = run_bass_kernel_spmd(nc, [arrays], core_ids=[0])
    return r.results[0]["out"]
```
